# Optimizing a Trainium2 kernel written in Bass

```python
import numpy as np
import jax
import jax.numpy as jnp

def _softmax(x, axis=-1):
    return jax.nn.softmax(x, axis=axis)

def _gelu(x):
    return jax.nn.gelu(x, approximate=True)

def _silu(x):
    return jax.nn.silu(x)

def _sigmoid(x):
    return jax.nn.sigmoid(x)

def _layernorm(x, axis=-1, eps=1e-05):
    m = jnp.mean(x, axis=axis, keepdims=True)
    v = jnp.var(x, axis=axis, keepdims=True)
    return (x - m) / jnp.sqrt(v + eps)

def _scatter_add(tgt, idx, src, axis=0):
    return tgt.at[idx].add(src)

def _segment_sum(src, seg, n):
    return jax.ops.segment_sum(src, seg, n)
kernel_name = 'mk_seq_preln_d1_jaxref_r4_c3c013'

def setup_inputs(seed: int=0):
    np.random.seed(seed)
    _w = jnp.asarray

    def _L0_attn_setup():
        import jax, jax.numpy as jnp
        import numpy as np
        B, T, C = (4, 512, 512)
        H = 32
        N = C // H
        N_LAYER = 12
        LAYER_ID = 6
        EPS = 1e-05 * 144
        key = jax.random.key(seed)
        ks = jax.random.split(key, 8)
        r01 = LAYER_ID / N_LAYER
        r1a0 = 1.0 - LAYER_ID / N_LAYER
        ddd = jnp.arange(C, dtype=jnp.float32) / C
        time_maa_k = (ddd ** r1a0).reshape(1, 1, C)
        time_maa_v = time_maa_k + 0.3 * r01
        time_maa_r = (ddd ** (0.5 * r1a0)).reshape(1, 1, C)
        time_maa_g = time_maa_r
        h = jnp.arange(H, dtype=jnp.float32) / (H - 1)
        time_decay = (-6.0 + 5.0 * h ** (0.7 + 0.3 * r01)).reshape(H, 1)
        zigzag = (((jnp.arange(H) + 1) % 3).astype(jnp.float32) - 1.0) * 0.1
        time_faaaa = (r01 * (1.0 - h) + zigzag).reshape(H, 1)

        def W(k):
            return jax.random.normal(k, (C, C), dtype=jnp.float32) * 0.02
        return {'x': jax.random.normal(ks[0], (B, T, C), dtype=jnp.float32), 'time_maa_k': time_maa_k, 'time_maa_v': time_maa_v, 'time_maa_r': time_maa_r, 'time_maa_g': time_maa_g, 'time_decay': time_decay, 'time_faaaa': time_faaaa, 'Wr': W(ks[1]), 'Wk': W(ks[2]), 'Wv': W(ks[3]), 'Wg': W(ks[4]), 'Wo': W(ks[5]), 'gamma': jnp.ones((C,), jnp.float32), 'beta': jnp.zeros((C,), jnp.float32)}
    _L0_attn_in = _L0_attn_setup()

    def _L0_ffn_setup():
        import jax, jax.numpy as jnp
        import numpy as np
        key = jax.random.key(seed)
        k1, k2, k3, k4, k5 = jax.random.split(key, 5)
        B, L, H, N = (2, 512, 512, 2048)
        x = jax.random.normal(k1, (B, L, H), dtype=jnp.float32)
        W0 = jax.random.normal(k2, (N, H), dtype=jnp.float32) * (1.0 / np.sqrt(H))
        bias0 = jax.random.normal(k3, (N,), dtype=jnp.float32) * 0.02
        W1 = jax.random.normal(k4, (H, N), dtype=jnp.float32) * (1.0 / np.sqrt(N))
        bias1 = jax.random.normal(k5, (H,), dtype=jnp.float32) * 0.02
        return {'x': x, 'W0': W0, 'bias0': bias0, 'W1': W1, 'bias1': bias1}
    _L0_ffn_in = _L0_ffn_setup()
    _d = {'L0_attn_x': _L0_attn_in['x'], 'L0_attn_time_maa_k': _L0_attn_in['time_maa_k'], 'L0_attn_time_maa_v': _L0_attn_in['time_maa_v'], 'L0_attn_time_maa_r': _L0_attn_in['time_maa_r'], 'L0_attn_time_maa_g': _L0_attn_in['time_maa_g'], 'L0_attn_time_decay': _L0_attn_in['time_decay'], 'L0_attn_time_faaaa': _L0_attn_in['time_faaaa'], 'L0_attn_Wr': _L0_attn_in['Wr'], 'L0_attn_Wk': _L0_attn_in['Wk'], 'L0_attn_Wv': _L0_attn_in['Wv'], 'L0_attn_Wg': _L0_attn_in['Wg'], 'L0_attn_Wo': _L0_attn_in['Wo'], 'L0_attn_gamma': _L0_attn_in['gamma'], 'L0_attn_beta': _L0_attn_in['beta'], 'L0_ffn_W0': _L0_ffn_in['W0'], 'L0_ffn_bias0': _L0_ffn_in['bias0'], 'L0_ffn_W1': _L0_ffn_in['W1'], 'L0_ffn_bias1': _L0_ffn_in['bias1']}
    _x0 = _d['L0_attn_x']
    _d['L0_attn_x'] = jax.random.normal(jax.random.fold_in(jax.random.key(seed), 1), (4, 2048, 512), dtype=_x0.dtype)
    del _x0
    return _d

def reference(L0_attn_x, L0_attn_time_maa_k, L0_attn_time_maa_v, L0_attn_time_maa_r, L0_attn_time_maa_g, L0_attn_time_decay, L0_attn_time_faaaa, L0_attn_Wr, L0_attn_Wk, L0_attn_Wv, L0_attn_Wg, L0_attn_Wo, L0_attn_gamma, L0_attn_beta, L0_ffn_W0, L0_ffn_bias0, L0_ffn_W1, L0_ffn_bias1):

    def _L0_attn_ref(x, time_maa_k, time_maa_v, time_maa_r, time_maa_g, time_decay, time_faaaa, Wr, Wk, Wv, Wg, Wo, gamma, beta):
        import jax, jax.numpy as jnp
        import numpy as np
        B, T, C = (4, 512, 512)
        H = 32
        N = C // H
        N_LAYER = 12
        LAYER_ID = 6
        EPS = 1e-05 * 144
        B, T, C = x.shape
        Hh = time_decay.shape[0]
        Nn = C // Hh
        Q = 64 if T % 64 == 0 else 128 if T % 128 == 0 else T
        nC = T // Q
        xx = jnp.pad(x, ((0, 0), (1, 0), (0, 0)))[:, :T] - x
        xk = x + xx * time_maa_k
        xv = x + xx * time_maa_v
        xr = x + xx * time_maa_r
        xg = x + xx * time_maa_g
        r = (xr @ Wr.T).reshape(B, T, Hh, Nn).transpose(0, 2, 1, 3)
        k = (xk @ Wk.T).reshape(B, T, Hh, Nn).transpose(0, 2, 3, 1)
        v = (xv @ Wv.T).reshape(B, T, Hh, Nn).transpose(0, 2, 1, 3)
        g = jax.nn.silu(xg @ Wg.T)
        w = jnp.exp(-jnp.exp(time_decay))
        u = time_faaaa
        ws = (w ** Q).reshape(1, Hh, 1, 1)
        qa = jnp.arange(Q)
        wk = (w ** (Q - 1 - qa)[None, :]).reshape(1, Hh, 1, Q)
        wb = (w ** qa[None, :]).reshape(1, Hh, Q, 1)
        i = qa[:, None]
        j = qa[None, :]
        pw = w.reshape(Hh, 1, 1) ** jnp.maximum(i - j - 1, 0)[None]
        w_mat = jnp.where(i > j, pw, jnp.where(i == j, u.reshape(Hh, 1, 1), jnp.zeros((), x.dtype))).reshape(1, Hh, Q, Q)
        rr = r.reshape(B, Hh, nC, Q, Nn).transpose(2, 0, 1, 3, 4)
        kk = k.reshape(B, Hh, Nn, nC, Q).transpose(3, 0, 1, 2, 4)
        vv = v.reshape(B, Hh, nC, Q, Nn).transpose(2, 0, 1, 3, 4)

        def step(state, inp):
            rc, kc, vc = inp
            att = rc @ kc * w_mat
            yc = att @ vc + rc @ state * wb
            new_state = ws * state + kc * wk @ vc
            return (new_state, yc)
        state0 = jnp.zeros((B, Hh, Nn, Nn), x.dtype)
        _, ys = jax.lax.scan(step, state0, (rr, kk, vv))
        y = ys.transpose(1, 0, 3, 2, 4).reshape(B, T, Hh, Nn)
        mu = jnp.mean(y, axis=-1, keepdims=True)
        var = jnp.mean(jnp.square(y - mu), axis=-1, keepdims=True)
        yn = ((y - mu) / jnp.sqrt(var + EPS)).reshape(B, T, C) * gamma + beta
        out = yn * g @ Wo.T
        return out

    def _L0_ffn_ref(x, W0, bias0, W1, bias1):
        import jax, jax.numpy as jnp
        import numpy as np
        B, L, H = x.shape
        X = x.reshape(-1, H).astype(jnp.float16)
        D = jnp.dot(X.astype(jnp.float32), W0.T) + bias0
        D = jax.nn.gelu(D, approximate=False).astype(jnp.float16)
        E = jnp.dot(D.astype(jnp.float32), W1.T) + bias1
        return E.astype(jnp.float16).reshape(B, L, H)
    x = L0_attn_x
    x = x + _L0_attn_ref(_layernorm(x, axis=-1), L0_attn_time_maa_k, L0_attn_time_maa_v, L0_attn_time_maa_r, L0_attn_time_maa_g, L0_attn_time_decay, L0_attn_time_faaaa, L0_attn_Wr, L0_attn_Wk, L0_attn_Wv, L0_attn_Wg, L0_attn_Wo, L0_attn_gamma, L0_attn_beta)
    x = x + _L0_ffn_ref(_layernorm(x, axis=-1), L0_ffn_W0, L0_ffn_bias0, L0_ffn_W1, L0_ffn_bias1)
    return x

_drawn_inputs = setup_inputs


def setup_inputs(seed=0):
    import zlib

    import numpy as np

    out = dict(_drawn_inputs(seed))
    spreads = {'L0_attn_gamma': (1.0, 0.6), 'L0_attn_beta': (0.0, 0.8)}
    factors = {'L0_attn_time_faaaa': 8.0, 'L0_ffn_bias0': 4.946, 'L0_ffn_bias1': 3.532}
    for name, (base, spread) in spreads.items():
        noise = np.random.default_rng([zlib.crc32(name.encode()), seed]).standard_normal(out[name].shape)
        drawn = base * np.exp(spread * noise) if base else spread * noise
        out[name] = jnp.asarray(drawn.astype(out[name].dtype))
    for name, factor in factors.items():
        out[name] = (out[name] * factor).astype(out[name].dtype)
    return out
```

```python
from contextlib import ExitStack

import numpy as np

import concourse.bass as bass
from concourse import mybir

F32, F16, I32 = mybir.dt.float32, mybir.dt.float16, mybir.dt.int32
ALU = mybir.AluOpType
ACT = mybir.ActivationFunctionType
AX = mybir.AxisListType

P = 128
C = 512
H, N = 32, 16
G = C // P
HID = 2048
Q = 64
BT, NT = 256, 2
NCH = BT // Q
T = 2048
FT, FN = 512, 4
LN_EPS = 1e-5
GN_EPS = 1e-5 * 144
KS = 2.0 ** 10
ATT_S = 2.0 ** -5
STATE_S = 2.0 ** -7
YG_S = 2.0 ** -1
EXP_BITS = 0x7F800000
RSQRT_MAGIC = 0x5F3759DF


class Step:

    def __init__(self, nc, ctx, name, per, unit=1, passed=None):
        self.sem = ctx.enter_context(nc.semaphore(name))
        self.per, self.unit = per, unit
        self.passed = passed

    def done(self, instruction):
        return instruction.then_inc(self.sem, self.unit)

    def wait(self, eng, block, k=None):
        value = (block * self.per + (self.per if k is None else k)) * self.unit
        if not isinstance(value, int) or value > 0:
            eng.wait_ge(self.sem, value)

    def wait_apart(self, eng, block, k=None):
        self.wait(eng, block, k)
        if not isinstance(block, int):
            eng.sem_inc(self.passed, 1)


def rsqrt(eng, step, block, x, y, t, first):
    k = [first]

    def then(instruction):
        step.done(instruction)
        k[0] += 1
        step.wait(eng, block, k[0])

    then(eng.tensor_scalar(t.bitcast(I32), x.bitcast(I32), 1, None, ALU.logical_shift_right))
    then(eng.tensor_scalar(y.bitcast(I32), t.bitcast(I32), -1.0, float(RSQRT_MAGIC), ALU.mult, ALU.add))
    for _ in range(3):
        then(eng.tensor_tensor(t, y, y, ALU.mult))
        then(eng.scalar_tensor_tensor(out=t, in0=t, scalar=-0.5, in1=x, op0=ALU.mult, op1=ALU.mult))
        then(eng.scalar_tensor_tensor(out=y, in0=t, scalar=1.5, in1=y, op0=ALU.add, op1=ALU.mult))


RSQRT_STEPS = 11


def load_weights(nc, ctx, tag, units, rho, scl, centre, ident16, centring):
    nu, nw = len(units), rho.shape[1]
    with ExitStack() as own:
        raw = own.enter_context(nc.sbuf_tensor(f"{tag}raw", [P, nu, G, C], F32))
        nat = own.enter_context(nc.sbuf_tensor(f"{tag}nat", [P, 2, 2, G, C], F16))
        junk = own.enter_context(nc.sbuf_tensor(f"{tag}junk", [P, G * C], F32))
        sums = own.enter_context(nc.sbuf_tensor(f"{tag}sums", [P, nu, G], F32))
        most = own.enter_context(nc.sbuf_tensor(f"{tag}most", [P, nw], F32))
        tps = own.enter_context(nc.psum_tensor(f"{tag}tps", [P, 4, 2 * C], F16))
        cps = own.enter_context(nc.psum_tensor(f"{tag}cps", [P, 4, C], F32))
        landed = [Step(nc, own, f"{tag}landed{u}", 1, 16) for u in range(nu)]
        s_cen = Step(nc, own, f"{tag}cen", 1)
        s_cent = Step(nc, own, f"{tag}cent", 1)
        s_sum = Step(nc, own, f"{tag}sum", 1)
        s_max = Step(nc, own, f"{tag}max", 1)
        s_all = Step(nc, own, f"{tag}all", 1)
        s_norm = Step(nc, own, f"{tag}norm", 1)
        s_scl = Step(nc, own, f"{tag}scl", 1)
        s_hi = Step(nc, own, f"{tag}hi", 1)
        s_lo = Step(nc, own, f"{tag}lo", 1)
        s_tr = Step(nc, own, f"{tag}tr", 4)
        s_evd = Step(nc, own, f"{tag}evd", 2)
        s_eva = Step(nc, own, f"{tag}eva", 2)
        cols = [c for _, c, _ in units]

        def evacuate(eng, u, hl, step):
            dst = units[u][2]
            for half in range(2):
                s_tr.wait(eng, u, 2 * hl + half + 1)
                out, src = dst[:, hl, 2 * half:2 * half + 2, :], tps[:, 2 * hl + half, :].rearrange(
                    "p (k c) -> p k c", k=2)
                step.done(eng.activation(out, src, ACT.Copy) if hl else eng.tensor_copy(out, src))

        with nc.Block() as block:

            @block.sync
            def _(eng):
                for u, (src, _, _) in enumerate(units):
                    landed[u].done(eng.dma_start(raw[:, u, :, :], src.rearrange("(b p) c -> p b c", p=P)))

            @block.scalar
            def _(eng):
                for u in range(nu):
                    landed[u].wait(eng, 0)
                    if u == centre:
                        s_cent.wait(eng, 0)
                    for b in range(G):
                        k = u * G + b
                        s_sum.wait(eng, k - 1)
                        s_sum.done(eng.activation(junk[:, 0:C], raw[:, u, b, :], ACT.Square,
                                                  accum_out=sums[:, u, b:b + 1]))
                s_all.wait(eng, 0)
                s_norm.done(eng.activation(rho, most[:, :], ACT.Sqrt))
                for u in range(nu):
                    s_scl.wait(eng, 3)
                    s_tr.wait(eng, u - 2)
                    s_hi.done(eng.activation(nat[:, u % 2, 0, :, :], raw[:, u, :, :], ACT.Identity,
                                             scale=scl[:, cols[u]:cols[u] + 1]))
                    if u:
                        evacuate(eng, u - 1, 1, s_eva)
                evacuate(eng, nu - 1, 1, s_eva)

            @block.gpsimd
            def _(eng):
                s_max.wait(eng, nw - 1)
                s_all.done(eng.partition_all_reduce(most[:, :], most[:, :], P, bass.bass_isa.ReduceOp.max))

            @block.vector
            def _(eng):
                if centre is not None:
                    s_cen.wait(eng, 0)
                    s_cent.done(eng.tensor_copy(raw[:, centre, :, :], cps[:, :, :]))
                for w in range(nw):
                    us = [u for u in range(nu) if cols[u] == w]
                    s_sum.wait(eng, us[-1] * G + G - 1)
                    s_max.done(eng.tensor_reduce(most[:, w:w + 1], sums[:, us[0]:us[-1] + 1, :], AX.XY, ALU.max))
                s_norm.wait(eng, 0)
                s_scl.done(eng.tensor_scalar(rho, rho, 1e-12, None, ALU.max))
                s_scl.wait(eng, 0)
                s_scl.done(eng.tensor_scalar(rho.bitcast(I32), rho.bitcast(I32), EXP_BITS, None, ALU.bitwise_and))
                s_scl.wait(eng, 1)
                s_scl.done(eng.reciprocal(scl, rho))
                s_scl.wait(eng, 2)
                s_scl.done(eng.tensor_scalar(scl, scl, KS, None, ALU.mult))
                for u in range(nu):
                    s_scl.wait(eng, 3)
                    s_hi.wait(eng, u)
                    s_lo.done(eng.scalar_tensor_tensor(
                        out=nat[:, u % 2, 1, :, :].rearrange("p b c -> p (b c)"),
                        in0=raw[:, u, :, :].rearrange("p b c -> p (b c)"),
                        scalar=scl[:, cols[u]:cols[u] + 1],
                        in1=nat[:, u % 2, 0, :, :].rearrange("p b c -> p (b c)"),
                        op0=ALU.mult, op1=ALU.subtract))
                    if u:
                        evacuate(eng, u - 1, 0, s_evd)
                evacuate(eng, nu - 1, 0, s_evd)

            @block.tensor
            def _(eng):
                if centre is not None:
                    landed[centre].wait(eng, 0)
                    for b in range(G):
                        mm = eng.matmul(cps[:, b, :], centring, raw[:, centre, b, :], start=True, stop=True)
                    s_cen.done(mm)
                for u in range(nu):
                    for hl in range(2):
                        (s_lo if hl else s_hi).wait(eng, u)
                        for half in range(2):
                            (s_eva if hl else s_evd).wait(eng, u - 1, half + 1)
                            for kk in range(2):
                                for b in range(G):
                                    k = 2 * half + kk
                                    tr = eng.transpose(tps[:, 2 * hl + half, kk * C + b * P:kk * C + (b + 1) * P],
                                                       nat[:, u % 2, hl, b, k * P:(k + 1) * P], ident16)
                            s_tr.done(tr)


def attention(nc, ctx, x, x1_out, maas, weights, decay, bonus, gamma, beta, consts, nb):

    def sb(name, shape, dt=F32):
        return ctx.enter_context(nc.sbuf_tensor(name, shape, dt))

    def ps(name, shape, dt=F32):
        return ctx.enter_context(nc.psum_tensor(name, shape, dt))

    s_passed = ctx.enter_context(nc.semaphore("a_passed"))

    def step(name, per, unit=1):
        return Step(nc, ctx, name, per, unit, s_passed)

    ident = sb("ident", [P, P])
    ident16 = sb("ident16", [P, P], F16)
    centring = sb("centring", [P, P])
    WT = sb("WT", [P, 5, 2, G, C], F16)
    rho = sb("rho", [P, 5])
    scl = sb("scl", [P, 5])
    maa = sb("maa", [P, 4, G])
    wmask = sb("wmask", [P, NT * 8, Q])
    headmask = sb("headmask", [P, P])
    wb = sb("wb", [P, H])
    wk = sb("wk", [P, H])
    ws = sb("ws", [P, G])
    flag = sb("flag", [P, nb + 1])
    gam = sb("gam", [P, G])
    bet = sb("bet", [P, G])
    gn_eps = sb("gn_eps", [P, 1])
    half_rho_g = sb("half_rho_g", [P, 1])
    out_scale = sb("out_scale", [P, 1])
    s_const = step("s_const", 1, 16)

    with nc.Block() as block:
        @block.sync
        def _(eng):
            s_const.done(eng.dma_start(ident[:, :], consts["ident"]))
            s_const.done(eng.dma_start(ident16[:, :], consts["ident16"]))
            s_const.done(eng.dma_start(centring[:, :], consts["centring"]))
            s_const.done(eng.dma_start(headmask[:, :], consts["headmask"]))
            s_const.wait(eng, 3)

    K_, R_, V_, G_, O_ = range(5)
    load_weights(nc, ctx, "a", [(weights[w], w, WT[:, w, :, :, :]) for w in range(5)],
                 rho[:, :], scl[:, :], V_, ident16[:, :], centring[:, :])

    with ExitStack() as own:
        def tb(name, shape):
            return own.enter_context(nc.sbuf_tensor(name, shape, F32))
        dist = tb("dist", [P, Q])
        after = tb("after", [P, Q])
        same = tb("same", [P, Q])
        ages = tb("ages", [P, 2])
        ep = tb("ep", [P, NT * 8])
        up = tb("up", [P, NT * 8])
        un = tb("un", [P, H])
        en = tb("en", [P, H])
        ec = tb("ec", [P, G])
        diag = tb("diag", [P, NT * 8, Q])
        s_in = Step(nc, own, "t_in", 1, 16)
        s_e = Step(nc, own, "t_e", 1)
        s_n = Step(nc, own, "t_n", 1)
        s_x = Step(nc, own, "t_x", 1)
        s_t = Step(nc, own, "t_t", 1)
        nin = 0
        with nc.Block() as block:
            loads = [(dist[:, :], consts["dist"]), (after[:, :], consts["after"]), (same[:, :], consts["same"]),
                     (ages[:, :], consts["ages"]),
                     (en[:, :], decay.rearrange("h o -> (h o)").partition_broadcast(P)),
                     (un[:, :], bonus.rearrange("h o -> (h o)").partition_broadcast(P))]
            for h in range(8):
                loads.append((ec[N * h:N * h + N, :],
                              decay.rearrange("(g h) o -> h (g o)", h=8)[h].partition_broadcast(N)))
            for m, v in enumerate(maas):
                loads.append((maa[:, m, :], v.rearrange("a b (g p) -> p (a b g)", p=P)))
            loads += [(gam[:, :], gamma.rearrange("(g p) -> p g", p=P)), (bet[:, :], beta.rearrange("(g p) -> p g", p=P))]
            nin = len(loads)

            @block.sync
            def _(eng):
                for dst, src in loads:
                    s_in.done(eng.dma_start(dst, src, allow_slow_non_contiguous=True))

            @block.scalar
            def _(eng):
                s_in.wait(eng, nin - 1)
                for t in (en, ec):
                    s_e.done(eng.activation(t[:, :], t[:, :], ACT.Exp))
                s_n.wait(eng, 5)
                for q in range(NT * 8):
                    s_x.done(eng.activation(wmask[:, q, :], dist[:, :], ACT.Exp, scale=ep[:, q:q + 1]))
                s_x.done(eng.activation(wb[:, :], wb[:, :], ACT.Exp))
                s_x.done(eng.activation(wk[:, :], wk[:, :], ACT.Exp))
                s_x.done(eng.activation(ws[:, :], ec[:, :], ACT.Exp, scale=-float(Q)))

            @block.vector
            def _(eng):
                nq = NT * 8
                s_in.wait(eng, nin - 1)
                s_e.wait(eng, 1)
                s_n.done(eng.tensor_scalar(wb[:, :], en[:, :], ages[:, 0:1], None, ALU.mult))
                s_n.done(eng.tensor_scalar(wk[:, :], en[:, :], ages[:, 1:2], None, ALU.mult))
                for p in range(2):
                    half = slice(Q * p, Q * p + Q)
                    s_n.done(eng.tensor_scalar(ep[half, :], en[half, p:H:2], -1.0, None, ALU.mult))
                    s_n.done(eng.tensor_copy(up[half, :], un[half, p:H:2]))
                s_n.wait(eng, 5)
                s_n.done(eng.tensor_tensor(diag[:, :, :], same[:, :].unsqueeze(1).to_broadcast([P, nq, Q]),
                                           up[:, :].unsqueeze(2).to_broadcast([P, nq, Q]), ALU.mult))
                s_x.wait(eng, nq + 2)
                s_t.done(eng.tensor_tensor(wmask[:, :, :], wmask[:, :, :],
                                           after[:, :].unsqueeze(1).to_broadcast([P, nq, Q]), ALU.mult))
                s_t.wait(eng, 0)
                s_n.wait(eng, 6)
                s_t.done(eng.tensor_tensor(wmask[:, :, :], wmask[:, :, :], diag[:, :, :], ALU.add))
                s_t.done(eng.tensor_scalar(wb[:, :], wb[:, :], ATT_S / STATE_S, None, ALU.mult))
                s_t.done(eng.tensor_scalar(wk[:, :], wk[:, :], STATE_S / KS, None, ALU.mult))
                s_t.done(eng.tensor_scalar(gam[:, :], gam[:, :], YG_S / (2 * KS), None, ALU.mult))
                s_t.done(eng.tensor_scalar(bet[:, :], bet[:, :], YG_S / (2 * KS), None, ALU.mult))
                s_t.done(eng.memset(flag[:, :], 1.0))
                s_t.wait(eng, 6)
                s_t.done(eng.memset(flag[:, 0:nb + 1:T // BT], 0.0))
                s_t.done(eng.tensor_tensor(gn_eps[:, :], rho[:, K_:K_ + 1], rho[:, R_:R_ + 1], ALU.mult))
                s_t.wait(eng, 8)
                s_t.done(eng.tensor_tensor(gn_eps[:, :], gn_eps[:, :], rho[:, V_:V_ + 1], ALU.mult))
                s_t.wait(eng, 9)
                s_t.done(eng.reciprocal(gn_eps[:, :], gn_eps[:, :]))
                s_t.wait(eng, 10)
                s_t.done(eng.tensor_tensor(gn_eps[:, :], gn_eps[:, :], gn_eps[:, :], ALU.mult))
                s_t.wait(eng, 11)
                s_t.done(eng.tensor_scalar(gn_eps[:, :], gn_eps[:, :], GN_EPS * ATT_S ** 2, None, ALU.mult))
                s_t.done(eng.tensor_scalar(half_rho_g[:, :], rho[:, G_:G_ + 1], 0.5 / KS, None, ALU.mult))
                s_t.done(eng.tensor_tensor(out_scale[:, :], rho[:, G_:G_ + 1], rho[:, O_:O_ + 1], ALU.mult))
                s_t.wait(eng, 14)
                s_t.done(eng.tensor_scalar(out_scale[:, :], out_scale[:, :], 1.0 / (KS * YG_S), None, ALU.mult))

    xa = sb("xa", [P, NT, C])
    bn = sb("bn", [P, NT, 6])
    mv = sb("mv", [P, NT, 2])
    ln_a, ln_r, ln_t, ln_n = (sb(f"ln_{c}", [P, NT]) for c in "artn")
    xnT = sb("xnT", [P, G, BT + 1])
    dx = sb("dx", [P, G, BT])
    mixf = sb("mixf", [P, 2, G, BT])
    mix = sb("mix", [P, 4, 2, G, BT], F16)
    kT = sb("kT", [P, 2, G, BT], F16)
    rT = sb("rT", [P, 2, G, BT], F16)
    kx = sb("kx", [P, 2 * G, NCH, 2, Q], F16)
    rx = sb("rx", [P, 2, G, 4, BT], F16)
    kN = sb("kN", [P, NT, 2, C], F16)
    vN = sb("vN", [P, NT, 2, 2, C // 2], F16)
    vw32 = sb("vw32", [P, NT, C])
    vw = sb("vw", [P, NT, 2, C], F16)
    vbd = sb("vbd", [P, NT, 2, 2, 2, C // 2], F16)
    tg = sb("tg", [P, NT, C])
    gT = sb("gT", [P, G, BT])
    att32 = sb("att32", [P, 2, C])
    att = sb("att", [P, 2, 2, 2 * C], F16)
    kv = sb("kv", [P, C])
    S = sb("S", [P, C])
    Sw = sb("Sw", [P, C])
    Shl = sb("Shl", [P, 2, 2, C], F16)
    yi = sb("yi", [P, C])
    y = sb("y", [P, NT, C])
    ysq = sb("ysq", [P, C])
    gn_s, gn_a, gn_r, gn_t = (sb(f"gn_{c}", [P, H]) for c in "sart")
    ygT = sb("ygT", [P, G, BT])
    yg = sb("yg", [P, 2, G, BT], F16)
    x1 = sb("x1", [P, NT, C])

    big = ps("big", [P, 2, C])
    sc = ps("sc", [P, 2, C])
    Y = ps("Y", [P, 2, C])
    kvp = ps("kvp", [P, C])
    trp = ps("trp", [P, 2 * C], F16)

    s_xa = step("s_xa", 1, 16)
    s_xr = step("s_xr", 1, 16)
    s_st = step("s_st", 1, 16)
    s_kx = step("s_kx", 8, 16)
    s_rx = step("s_rx", 4, 16)
    s_vbd = [step(f"s_vbd{t}", 4, 16) for t in range(NT)]
    s_bn = step("s_bn", 4)
    s_ln = step("s_ln", 2 + RSQRT_STEPS)
    s_xn = step("s_xn", NT)
    s_X = step("s_X", NT)
    s_xT = step("s_xT", NT)
    s_carry = step("s_carry", 1)
    s_dx = step("s_dx", 1)
    s_mix = step("s_mix", 4)
    s_mh = step("s_mh", 4)
    s_ml = step("s_ml", 4)
    s_pK = step("s_pK", 2)
    s_pR = step("s_pR", 2)
    s_pG = step("s_pG", 2)
    s_pV = step("s_pV", NT)
    s_kh = step("s_kh", 2)
    s_kl = step("s_kl", 2)
    s_rh = step("s_rh", 2)
    s_rl = step("s_rl", 2)
    s_vh = step("s_vh", NT)
    s_vl = step("s_vl", NT)
    s_vw = step("s_vw", NT)
    s_vwh = step("s_vwh", NT)
    s_vwl = step("s_vwl", NT)
    s_kt = step("s_kt", NT)
    s_kN = step("s_kN", NT)
    s_tg = step("s_tg", 2)
    s_gT = step("s_gT", 2)
    s_sc = step("s_sc", 2 * NCH)
    s_am = step("s_am", 2 * NCH)
    s_ah = step("s_ah", 2 * NCH)
    s_al = step("s_al", 2 * NCH)
    s_av = step("s_av", NCH)
    s_in = step("s_in", NCH)
    s_kv = step("s_kv", NCH)
    s_km = step("s_km", NCH)
    s_S = step("s_S", NCH)
    s_Sf = step("s_Sf", 1)
    s_Sh = step("s_Sh", NCH)
    s_Sl = step("s_Sl", NCH)
    s_Sw = step("s_Sw", NCH)
    s_yi = step("s_yi", NT)
    s_y = step("s_y", NT)
    s_sq = step("s_sq", NT)
    s_gs = step("s_gs", NT)
    s_gn = step("s_gn", NT * (1 + RSQRT_STEPS))
    s_yn = step("s_yn", NT)
    s_yT = step("s_yT", NT)
    s_af = step("s_af", NT * G)
    s_yg = step("s_yg", NT)
    s_ygh = step("s_ygh", NT)
    s_ygl = step("s_ygl", NT)
    s_Wo = step("s_Wo", NT)
    s_x1 = step("s_x1", NT)
    s_zero = step("s_zero", 1)

    def split3(hl_pairs=((0, 0), (0, 1), (1, 0))):
        return hl_pairs

    def rows(t):
        return slice(P * t, P * t + P)


    def pe_project_T(eng, w, m, n, half, bank):
        for gg in range(2):
            g = 2 * half + gg
            for i, (a, b) in enumerate(split3()):
                for kk in range(G):
                    mm = eng.matmul(big[:, bank, gg * BT:(gg + 1) * BT], WT[:, w, a, kk, rows(g)],
                                    mix[:, m, b, kk, :], start=(i == 0 and kk == 0), stop=(i == 2 and kk == G - 1))
        return mm

    def pe_ahead_X(eng, n):
        for t in range(NT):
            s_xn.wait(eng, n, t + 1)
            if t == 0:
                s_vl.wait(eng, n - 1, 1)
            else:
                s_vl.wait(eng, n - 1, 2)
            for g in range(G):
                tr = eng.transpose(big[:, t, rows(g)], xa[:, t, rows(g)], ident[:, :])
            s_X.done(tr)

    def pe_tail_yT(eng, n):
        for t in range(NT):
            s_yn.wait(eng, n, t + 1)
            for g in range(G):
                tr = eng.transpose(big[:, t, rows(g)], y[:, t, rows(g)], ident[:, :])
            s_yT.done(tr)

    def pe_tail_Wo(eng, n, t):
        s_ygl.wait(eng, n, t + 1)
        for i, (a, b) in enumerate(split3()):
            for kk in range(G):
                mm = eng.matmul(big[:, 1, :], yg[:, a, kk, rows(t)], WT[:, 4, b, kk, :],
                                start=(i == 0 and kk == 0), stop=(i == 2 and kk == G - 1))
        s_Wo.done(mm)

    def pe_block(eng, n, tail, ahead):
        for half in range(2):
            if half == 0:
                s_gT.wait(eng, n - 1, 2)
            else:
                s_mix.wait(eng, n, 3)
            s_ml.wait(eng, n, 1)
            s_mh.wait(eng, n, 1)
            s_xT.wait(eng, n)
            s_pK.done(pe_project_T(eng, 0, 0, n, half, half))
        for half in range(2):
            s_ml.wait(eng, n, 2)
            s_mh.wait(eng, n, 2)
            s_kl.wait(eng, n, half + 1)
            s_pR.done(pe_project_T(eng, 1, 1, n, half, half))
        s_rl.wait(eng, n)
        if tail:
            pe_tail_yT(eng, n - 1)
            s_af.wait(eng, n - 1)
        s_ml.wait(eng, n, 3)
        s_mh.wait(eng, n, 3)
        for t in range(NT):
            for i, (a, b) in enumerate(split3()):
                for kk in range(G):
                    mm = eng.matmul(big[:, t, :], mix[:, 2, a, kk, rows(t)], WT[:, 2, b, kk, :],
                                    start=(i == 0 and kk == 0), stop=(i == 2 and kk == G - 1))
            s_pV.done(mm)
        for t in range(NT):
            s_kN.wait(eng, n - 1) if t == 0 else s_kN.wait(eng, n, 1)
            s_kl.wait(eng, n)
            for hl in range(2):
                for g in range(G):
                    tr = eng.transpose(trp[:, hl * C + g * P:hl * C + (g + 1) * P], kT[:, hl, g, rows(t)],
                                       ident16[:, :])
            s_kt.done(tr)
        if ahead:
            pe_ahead_X(eng, n + 1)
            s_xT.wait(eng, n + 1)
        else:
            s_vl.wait(eng, n)

        def scores(c):
            if c == 0:
                s_kx.wait(eng, n)
                s_rx.wait(eng, n)
            for x in range(2):
                s_am.wait(eng, n, 2 * (c - 1) + x + 1) if c else s_am.wait(eng, n - 1, 2 * (NCH - 1) + x + 1)
                for gg in range(2):
                    g = 2 * x + gg
                    for i, (a, b) in enumerate(split3()):
                        mm = eng.matmul(sc[:, x, gg * BT:(gg + 1) * BT], kx[:, G * a + g, c, :, :].rearrange("p a j -> p (a j)"),
                                        rx[:, b, g, :, Q * c:Q * c + Q], start=(i == 0), stop=(i == 2))
                s_sc.done(mm)

        def att_v(c):
            t, cc = c // 2, c % 2
            out = Y[Q * cc:Q * cc + Q, 0, :]
            if cc == 0:
                s_y.wait(eng, n, t) if t else s_y.wait(eng, n - 1)
                s_vbd[t].wait(eng, n)
            s_al.wait(eng, n, 2 * c + 2)
            for q in range(16):
                for i, (a, b) in enumerate(split3()):
                    mm = eng.matmul(out[:, 2 * N * q:2 * N * (q + 1)], att[:, cc, a, Q * q:Q * q + Q],
                                    vbd[:, t, cc, b, :, N * q:N * q + N],
                                    start=(i == 0), stop=(i == 2))
            s_av.done(mm)

        def from_state(c):
            t, cc = c // 2, c % 2
            if cc == 0:
                s_yi.wait(eng, n, t) if t else s_yi.wait(eng, n - 1)
            s_Sl.wait(eng, n, c) if c else s_Sl.wait(eng, n - 1)
            for g in range(G):
                for i, (a, b) in enumerate(split3()):
                    mm = eng.matmul(Y[Q * cc:Q * cc + Q, 1, rows(g)], rT[:, a, g, Q * c:Q * c + Q],
                                    Shl[:, cc, b, rows(g)], start=(i == 0), stop=(i == 2))
            s_in.done(mm)

        def kv_sum(c):
            t, cc = c // 2, c % 2
            s_km.wait(eng, n, c) if c else s_km.wait(eng, n - 1)
            if cc == 0:
                s_vwl.wait(eng, n, t + 1)
                s_vwh.wait(eng, n, t + 1)
                s_kN.wait(eng, n, t + 1)
            part = slice(Q * cc, Q * cc + Q)
            for g in range(G):
                for i, (a, b) in enumerate(split3()):
                    mm = eng.matmul(kvp[:, rows(g)], kN[part, t, a, rows(g)], vw[part, t, b, rows(g)],
                                    start=(i == 0), stop=(i == 2))
            s_kv.done(mm)

        def gate(half):
            if half == 0:
                s_ml.wait(eng, n, 4)
                s_mh.wait(eng, n, 4)
            else:
                s_gT.wait(eng, n, 1)
            s_pG.done(pe_project_T(eng, 3, 3, n, half, 0))

        scores(0)
        kv_sum(0)
        gate(0)
        scores(1)
        if tail:
            pe_tail_Wo(eng, n - 1, 0)
        att_v(0)
        from_state(0)
        kv_sum(1)
        gate(1)
        scores(2)
        if tail:
            s_x1.wait(eng, n - 1, 1)
            pe_tail_Wo(eng, n - 1, 1)
        att_v(1)
        from_state(1)
        kv_sum(2)
        scores(3)
        att_v(2)
        from_state(2)
        kv_sum(3)
        att_v(3)
        from_state(3)

    def dve_ln(eng, n):
        s_xa.wait(eng, n)
        for t in range(NT):
            s_bn.done(eng.bn_stats(bn[:, t, :], xa[:, t, :]))
        for t in range(NT):
            s_bn.wait_apart(eng, n, t + 1)
            s_bn.done(eng.bn_aggr(mv[:, t, :], bn[:, t, :]))
        s_bn.wait(eng, n)
        s_ln.done(eng.tensor_scalar(ln_a[:, :], mv[:, :, 1], LN_EPS, None, ALU.add))
        s_ln.wait(eng, n, 1)
        rsqrt(eng, s_ln, n, ln_a[:, :], ln_r[:, :], ln_t[:, :], 1)
        s_ln.done(eng.scalar_tensor_tensor(out=ln_n[:, :], in0=mv[:, :, 0], scalar=-1.0, in1=ln_r[:, :],
                                           op0=ALU.mult, op1=ALU.mult))

    def dve_dx(eng, n):
        s_xT.wait(eng, n)
        s_carry.wait(eng, n)
        s_dx.done(eng.tensor_tensor(dx[:, :, :], xnT[:, :, 0:BT], xnT[:, :, 1:BT + 1], ALU.subtract))

    def dve_carry(eng, n):
        s_mix.wait(eng, n - 1)
        s_carry.done(eng.tensor_scalar(xnT[:, :, 0:1], xnT[:, :, BT:BT + 1], flag[:, bass.ds(n, 1)],
                                       None, ALU.mult))

    def dve_mix(eng, n, m):
        if m == 0:
            s_dx.wait(eng, n)
        s_ml.wait(eng, n, m - 1) if m >= 2 else s_ml.wait(eng, n - 1, m + 3)
        for g in range(G):
            last = eng.scalar_tensor_tensor(out=mixf[:, m % 2, g, :], in0=dx[:, g, :], scalar=maa[:, m, g:g + 1],
                                            in1=xnT[:, g, 1:BT + 1], op0=ALU.mult, op1=ALU.add)
        s_mix.done(last)

    def dve_lo(eng, bank, hi, lo):
        return eng.scalar_tensor_tensor(out=lo, in0=big[:, bank, :].rearrange("p (g t) -> p g t", g=2),
                                        scalar=1.0 / KS, in1=hi, op0=ALU.mult, op1=ALU.subtract)

    def dve_block(eng, n, tail, ahead):
        if ahead:
            dve_carry(eng, n + 1)
            dve_ln(eng, n + 1)
        for half in range(2):
            s_kh.wait(eng, n, half + 1)
            g2 = slice(2 * half, 2 * half + 2)
            s_kl.done(dve_lo(eng, half, kT[:, 0, g2, :], kT[:, 1, g2, :]))
        for half in range(2):
            s_rh.wait(eng, n, half + 1)
            g2 = slice(2 * half, 2 * half + 2)
            s_rl.done(dve_lo(eng, half, rT[:, 0, g2, :], rT[:, 1, g2, :]))
        if tail:
            for t in range(NT):
                s_af.wait(eng, n - 1, G * (t + 1))
                s_yg.done(eng.tensor_tensor(ygT[:, :, rows(t)], ygT[:, :, rows(t)], gT[:, :, rows(t)], ALU.mult))
                s_ygh.wait(eng, n - 1, t + 1)
                s_ygl.done(eng.tensor_tensor(yg[:, 1, :, rows(t)], ygT[:, :, rows(t)], yg[:, 0, :, rows(t)],
                                             ALU.subtract))
        for t in range(NT):
            s_pV.wait(eng, n, t + 1)
            s_vw.done(eng.tensor_tensor(vw32[:, t, :].rearrange("p (h d) -> p h d", h=H),
                                        big[:, t, :].rearrange("p (h d) -> p h d", h=H),
                                        wk[:, :].unsqueeze(2).to_broadcast([P, H, N]), ALU.mult))
            s_vh.wait(eng, n, t + 1)
            for p in range(2):
                last = eng.scalar_tensor_tensor(
                    out=vN[:, t, 1, p, :].rearrange("p (q d) -> p q d", d=N),
                    in0=big[:, t, :].rearrange("p (q a d) -> p a q d", a=2, d=N)[:, p], scalar=1.0 / KS,
                    in1=vN[:, t, 0, p, :].rearrange("p (q d) -> p q d", d=N), op0=ALU.mult, op1=ALU.subtract)
            s_vl.done(last)

        def weigh(c):
            for x in range(2):
                s_sc.wait(eng, n, 2 * c + x + 1)
                s_al.wait(eng, n, 2 * c - 1 + x) if c else s_al.wait(eng, n - 1, 2 * NCH - 1 + x)
                s_am.done(eng.tensor_tensor(att32[:, x, :], sc[:, x, :],
                                            wmask[:, 8 * x:8 * x + 8, :].rearrange("p q i -> p (q i)"), ALU.mult))
            for x in range(2):
                s_ah.wait(eng, n, 2 * c + x + 1)
                s_al.done(eng.tensor_tensor(att[:, c % 2, 1, C * x:C * x + C], att32[:, x, :],
                                            att[:, c % 2, 0, C * x:C * x + C], ALU.subtract))

        def state(c):
            s_kv.wait(eng, n, c + 1)
            s_km.done(eng.tensor_tensor(kv[:, :].rearrange("p (g c) -> p g c", g=G),
                                        kvp[:, :].rearrange("p (g c) -> p g c", g=G),
                                        headmask[:, :].unsqueeze(1).to_broadcast([P, G, P]), ALU.mult))
            s_km.wait(eng, n, c + 1)
            s_Sw.wait(eng, n, c) if c else s_Sw.wait(eng, n - 1)
            s_Sl.wait(eng, n, c) if c else s_Sl.wait(eng, n - 1)
            s_S.done(eng.tensor_tensor(S[:, :], kv[:, :], Sw[:, :], ALU.add))
            if c == NCH - 1:
                s_S.wait(eng, n, c + 1)
                s_Sf.done(eng.tensor_scalar(S[:, :], S[:, :], flag[:, bass.ds(n + 1, 1)], None, ALU.mult))

        def state_lo(c):
            s_Sh.wait(eng, n, c + 1)
            b = (c + 1) % 2
            s_Sl.done(eng.tensor_tensor(Shl[:, b, 1, :], S[:, :], Shl[:, b, 0, :], ALU.subtract))

        def gate(half):
            s_tg.wait(eng, n, half + 1)
            g2 = slice(2 * half, 2 * half + 2)
            s_gT.done(eng.scalar_tensor_tensor(out=gT[:, g2, :], in0=tg[:, half, :].rearrange("p (g t) -> p g t", g=2),
                                               scalar=1.0, in1=big[:, 0, :].rearrange("p (g t) -> p g t", g=2),
                                               op0=ALU.add, op1=ALU.mult))

        def residual(t):
            s_xr.wait(eng, n - 1)
            s_Wo.wait(eng, n - 1, t + 1)
            s_x1.done(eng.scalar_tensor_tensor(out=x1[:, t, :], in0=big[:, 1, :], scalar=out_scale[:, 0:1],
                                               in1=x1[:, t, :], op0=ALU.mult, op1=ALU.add))

        def take_y(t):
            s_in.wait(eng, n, 2 * t + 2)
            s_av.wait(eng, n, 2 * t + 2)
            s_yi.done(eng.tensor_tensor(yi[:, :].rearrange("p (h d) -> p h d", h=H),
                                        Y[:, 1, :].rearrange("p (h d) -> p h d", h=H),
                                        wb[:, :].unsqueeze(2).to_broadcast([P, H, N]), ALU.mult))
            s_yi.wait(eng, n, t + 1)
            s_yT.wait(eng, n - 1)
            s_y.done(eng.tensor_tensor(y[:, t, :], Y[:, 0, :], yi[:, :], ALU.add))

        def normalize(t):
            k0 = t * (1 + RSQRT_STEPS)
            s_sq.wait(eng, n, t + 1)
            s_gs.done(eng.tensor_reduce(gn_s[:, :], ysq[:, :].rearrange("p (h d) -> p h d", h=H), AX.X, ALU.add))
            s_gs.wait(eng, n, t + 1)
            s_gn.done(eng.tensor_scalar(gn_a[:, :], gn_s[:, :], 1.0 / N, gn_eps[:, 0:1], ALU.mult, ALU.add))
            s_gn.wait(eng, n, k0 + 1)
            rsqrt(eng, s_gn, n, gn_a[:, :], gn_r[:, :], gn_t[:, :], k0 + 1)
            s_yn.done(eng.tensor_tensor(y[:, t, :].rearrange("p (h d) -> p h d", h=H),
                                        y[:, t, :].rearrange("p (h d) -> p h d", h=H),
                                        gn_r[:, :].unsqueeze(2).to_broadcast([P, H, N]), ALU.mult))

        weigh(0)
        if ahead:
            dve_dx(eng, n + 1)
            dve_mix(eng, n + 1, 0)
        state(0)
        gate(0)
        state_lo(0)
        weigh(1)
        if tail:
            residual(0)
        if ahead:
            dve_mix(eng, n + 1, 1)
        state(1)
        state_lo(1)
        weigh(2)
        gate(1)
        take_y(0)
        if tail:
            residual(1)
        if ahead:
            dve_mix(eng, n + 1, 2)
        state(2)
        state_lo(2)
        weigh(3)
        normalize(0)
        if ahead:
            dve_mix(eng, n + 1, 3)
        state(3)
        state_lo(3)
        take_y(1)
        normalize(1)

    def act_norm(eng, n):
        s_ln.wait(eng, n)
        for t in range(NT):
            s_xn.done(eng.activation(xa[:, t, :], xa[:, t, :], ACT.Identity, bias=ln_n[:, t:t + 1],
                                     scale=ln_r[:, t:t + 1]))

    def act_xT(eng, n):
        s_dx.wait(eng, n - 1)
        s_mix.wait(eng, n - 1)
        s_carry.wait(eng, n)
        for t in range(NT):
            s_X.wait(eng, n, t + 1)
            s_xT.done(eng.activation(xnT[:, :, 1 + P * t:1 + P * t + P],
                                     big[:, t, :].rearrange("p (g t) -> p g t", g=G), ACT.Copy))

    def act_mix_hi(eng, n, m):
        s_mix.wait(eng, n, m + 1)
        (s_pK, s_pR, s_pV, s_pG)[m].wait(eng, n - 1)
        s_mh.done(eng.activation(mix[:, m, 0, :, :], mixf[:, m % 2, :, :], ACT.Copy))

    def act_block(eng, n, tail, ahead):
        def project_hi(projected, done, dst, half, free):
            projected.wait(eng, n, half + 1)
            done.done(eng.activation(dst[:, 0, 2 * half:2 * half + 2, :],
                                     big[:, half, :].rearrange("p (g t) -> p g t", g=2), ACT.Copy, scale=1.0 / KS))

        s_kx.wait(eng, n - 1)
        s_kt.wait(eng, n - 1)
        for half in range(2):
            project_hi(s_pK, s_kh, kT, half, None)
        if ahead:
            act_norm(eng, n + 1)
        s_rx.wait(eng, n - 1)
        s_in.wait(eng, n - 1)
        for half in range(2):
            project_hi(s_pR, s_rh, rT, half, None)
        if tail:
            s_mix.wait(eng, n, 1)
            for t in range(NT):
                s_yT.wait(eng, n - 1, t + 1)
                for g in range(G):
                    s_af.done(eng.activation(ygT[:, g, rows(t)], big[:, t, rows(g)], ACT.Identity,
                                             bias=bet[:, g:g + 1], scale=gam[:, g:g + 1]))
            s_in.wait(eng, n - 1)
            for t in range(NT):
                s_yg.wait(eng, n - 1, t + 1)
                s_ygh.done(eng.activation(yg[:, 0, :, rows(t)], ygT[:, :, rows(t)], ACT.Copy))
        for t in range(NT):
            s_vbd[t].wait(eng, n - 1)
            s_vw.wait(eng, n, t + 1)
            s_vh.done(eng.activation(vN[:, t, 0, :, :].rearrange("p a (q d) -> p a q d", d=N),
                                     big[:, t, :].rearrange("p (q a d) -> p a q d", a=2, d=N), ACT.Copy,
                                     scale=1.0 / KS))
            s_kv.wait(eng, n - 1)
            s_vwh.done(eng.activation(vw[:, t, 0, :], vw32[:, t, :], ACT.Copy))
        for t in range(NT):
            s_kt.wait(eng, n, t + 1)
            s_kN.done(eng.activation(kN[:, t, :, :], trp[:, :].rearrange("p (a c) -> p a c", a=2), ACT.Copy))
        if ahead:
            act_xT(eng, n + 1)

        def weights_hi(c):
            s_av.wait(eng, n, c - 1) if c >= 2 else s_av.wait(eng, n - 1, NCH - 1 + c)
            for x in range(2):
                s_am.wait(eng, n, 2 * c + x + 1)
                s_ah.done(eng.activation(att[:, c % 2, 0, C * x:C * x + C], att32[:, x, :], ACT.Copy))

        def state_hi(c):
            b = (c + 1) % 2
            s_S.wait(eng, n, c + 1)
            if c == NCH - 1:
                s_Sf.wait(eng, n)
            s_in.wait(eng, n, c) if c else s_in.wait(eng, n - 1)
            s_Sh.done(eng.activation(Shl[:, b, 0, :], S[:, :], ACT.Copy))

        def gate(half):
            s_pG.wait(eng, n, half + 1)
            s_gT.wait(eng, n - 1)
            s_tg.done(eng.activation(tg[:, half, :], big[:, 0, :], ACT.Tanh, scale=half_rho_g[:, 0:1]))

        def square(t):
            s_y.wait(eng, n, t + 1)
            s_gs.wait(eng, n, t) if t else s_gs.wait(eng, n - 1)
            s_sq.done(eng.activation(ysq[:, :], y[:, t, :], ACT.Square))

        weights_hi(0)
        if ahead:
            act_mix_hi(eng, n + 1, 0)
        gate(0)
        state_hi(0)
        weights_hi(1)
        if ahead:
            act_mix_hi(eng, n + 1, 1)
        state_hi(1)
        weights_hi(2)
        gate(1)
        square(0)
        if ahead:
            act_mix_hi(eng, n + 1, 2)
        state_hi(2)
        weights_hi(3)
        if ahead:
            act_mix_hi(eng, n + 1, 3)
        state_hi(3)
        square(1)

    def pool_mix_lo(eng, n, m):
        s_mh.wait(eng, n, m + 1)
        s_ml.done(eng.tensor_tensor(mix[:, m, 1, :, :], mixf[:, m % 2, :, :], mix[:, m, 0, :, :], ALU.subtract))

    def pool_block(eng, n, tail, ahead):
        def decay_state(c):
            s_S.wait(eng, n, c + 1)
            if c == NCH - 1:
                s_Sf.wait(eng, n)
            s_Sw.done(eng.tensor_tensor(Sw[:, :].rearrange("p (g c) -> p g c", g=G),
                                        S[:, :].rearrange("p (g c) -> p g c", g=G),
                                        ws[:, :].unsqueeze(2).to_broadcast([P, G, P]), ALU.mult))

        for t in range(NT):
            s_vwh.wait(eng, n, t + 1)
            s_vwl.done(eng.tensor_tensor(vw[:, t, 1, :], vw32[:, t, :], vw[:, t, 0, :], ALU.subtract))
        for c in range(NCH):
            if ahead:
                pool_mix_lo(eng, n + 1, c)
            decay_state(c)

    def x_rows(x, n):
        return x[bass.ds(n * NT, NT), :, :].rearrange("t p c -> p t c")

    def sp_block(eng, n, tail, ahead, load):
        s_sc.wait_apart(eng, n - 1)
        s_kl.wait_apart(eng, n)
        for b in range(8):
            p = b % 2
            s_kx.done(eng.dma_start(kx[N * b:N * b + N, :, :, p, :],
                                    kT[N * b:N * b + N, :, :, :].rearrange("p a g (c j) -> p (a g) c j", j=Q)))
        s_rl.wait_apart(eng, n)
        for q in range(4):
            s_rx.done(eng.dma_start(rx[32 * q:32 * q + 32, :, :, q, :], rT[32 * q:32 * q + 32, :, :, :]))
        for t in range(NT):
            s_vl.wait_apart(eng, n, t + 1)
            s_av.wait_apart(eng, n - 1, 2 * t + 2)
            for c in range(2):
                for p in range(2):
                    s_vbd[t].done(eng.dma_start(vbd[Q * p:Q * p + Q, t, c, :, p, :], vN[Q * c:Q * c + Q, t, :, p, :]))
        if load:
            s_X.wait_apart(eng, n + 1)
            s_xa.done(eng.dma_start(xa[:, :, :], x_rows(x, n + 2)))
        if tail:
            s_x1.wait_apart(eng, n - 1)
            s_st.done(eng.dma_start(x_rows(x1_out, n - 1), x1[:, :, :]))
            s_st.wait_apart(eng, n - 1)
        s_xr.done(eng.dma_start(x1[:, :, :], x_rows(x, n)))

    def every_block(eng, block_fn, extra=False):
        if extra:
            block_fn(eng, 0, False, True, True)
            with eng.Fori(1, nb - 2) as n:
                block_fn(eng, n, True, True, True)
            block_fn(eng, nb - 2, True, True, False)
            block_fn(eng, nb - 1, True, False, False)
        else:
            block_fn(eng, 0, False, True)
            with eng.Fori(1, nb - 1) as n:
                block_fn(eng, n, True, True)
            block_fn(eng, nb - 1, True, False)

    with nc.Block() as block:
        @block.sync
        def _(eng):
            s_xa.done(eng.dma_start(xa[:, :, :], x_rows(x, 0)))
            s_X.wait(eng, 0)
            s_xa.done(eng.dma_start(xa[:, :, :], x_rows(x, 1)))
            s_zero.wait(eng, 2)
            every_block(eng, sp_block, True)
            s_x1.wait(eng, nb - 1)
            s_st.done(eng.dma_start(x_rows(x1_out, nb - 1), x1[:, :, :]))
            s_st.wait(eng, nb - 1)

        @block.tensor
        def _(eng):
            pe_ahead_X(eng, 0)
            s_zero.wait(eng, 4)
            every_block(eng, pe_block)
            pe_tail_yT(eng, nb - 1)
            pe_tail_Wo(eng, nb - 1, 0)
            s_x1.wait(eng, nb - 1, 1)
            pe_tail_Wo(eng, nb - 1, 1)

        @block.vector
        def _(eng):
            s_zero.done(eng.memset(kx[:, :, :, :, :].rearrange("p a c b t -> p (a c b t)").bitcast(F32), 0.0))
            s_zero.done(eng.memset(rx[:, :, :, :, :].rearrange("p a g b t -> p (a g b t)").bitcast(F32), 0.0))
            s_zero.done(eng.memset(vbd[:, :, :, :, :, :].rearrange("p t c a b d -> p (t c a b d)").bitcast(F32), 0.0))
            s_zero.done(eng.memset(Sw[:, :], 0.0))
            s_zero.done(eng.memset(Shl[:, 0, :, :].rearrange("p a c -> p (a c)").bitcast(F32), 0.0))
            dve_ln(eng, 0)
            s_carry.done(eng.memset(xnT[:, :, 0:1], 0.0))
            dve_dx(eng, 0)
            for m in range(4):
                dve_mix(eng, 0, m)
            every_block(eng, dve_block)
            for t in range(NT):
                s_af.wait(eng, nb - 1, G * (t + 1))
                s_yg.done(eng.tensor_tensor(ygT[:, :, rows(t)], ygT[:, :, rows(t)], gT[:, :, rows(t)], ALU.mult))
                s_ygh.wait(eng, nb - 1, t + 1)
                s_ygl.done(eng.tensor_tensor(yg[:, 1, :, rows(t)], ygT[:, :, rows(t)], yg[:, 0, :, rows(t)],
                                             ALU.subtract))
            for t in range(NT):
                s_xr.wait(eng, nb - 1)
                s_Wo.wait(eng, nb - 1, t + 1)
                s_x1.done(eng.scalar_tensor_tensor(out=x1[:, t, :], in0=big[:, 1, :], scalar=out_scale[:, 0:1],
                                                   in1=x1[:, t, :], op0=ALU.mult, op1=ALU.add))

        @block.scalar
        def _(eng):
            act_norm(eng, 0)
            act_xT(eng, 0)
            for m in range(4):
                act_mix_hi(eng, 0, m)
            every_block(eng, act_block)
            s_ygl.wait(eng, nb - 2)
            for t in range(NT):
                s_yT.wait(eng, nb - 1, t + 1)
                for g in range(G):
                    s_af.done(eng.activation(ygT[:, g, rows(t)], big[:, t, rows(g)], ACT.Identity,
                                             bias=bet[:, g:g + 1], scale=gam[:, g:g + 1]))
            s_Wo.wait(eng, nb - 2)
            for t in range(NT):
                s_yg.wait(eng, nb - 1, t + 1)
                s_ygh.done(eng.activation(yg[:, 0, :, rows(t)], ygT[:, :, rows(t)], ACT.Copy))

        @block.gpsimd
        def _(eng):
            for m in range(4):
                pool_mix_lo(eng, 0, m)
            every_block(eng, pool_block)


def ffn(nc, ctx, xio_in, out, W0, bias0, W1, bias1, consts, nb):

    def sb(name, shape, dt=F32):
        return ctx.enter_context(nc.sbuf_tensor(name, shape, dt))

    def ps(name, shape, dt=F32):
        return ctx.enter_context(nc.psum_tensor(name, shape, dt))

    s_passed = ctx.enter_context(nc.semaphore("f_passed"))

    def step(name, per, unit=1):
        return Step(nc, ctx, name, per, unit, s_passed)

    def rows(t):
        return slice(P * t, P * t + P)

    NH = HID // P
    ident16 = sb("f_ident16", [P, P], F16)
    W0T = sb("W0T", [P, 2, G, HID], F16)
    W1T = sb("W1T", [P, 2, NH, C], F16)
    rho = sb("f_rho", [P, 2])
    scl = sb("f_scl", [P, 2])
    b0 = sb("b0", [P, NH])
    b1 = sb("b1", [P, C])
    f_const = step("f_const", 1, 16)
    f_scale = step("f_scale", 1)
    with nc.Block() as block:
        @block.sync
        def _(eng):
            f_const.done(eng.dma_start(ident16[:, :], consts["ident16"]))
            f_const.done(eng.dma_start(b0[:, :], bias0.rearrange("(g p) -> p g", p=P),
                                       allow_slow_non_contiguous=True))
            f_const.done(eng.dma_start(b1[:, :], bias1.partition_broadcast(P)))
            f_const.wait(eng, 2)
    units = [(W0[C * u:C * u + C, :], 0, W0T[:, :, :, C * u:C * u + C]) for u in range(4)]
    units += [(W1[:, C * u:C * u + C], 1, W1T[:, :, G * u:G * u + G, :]) for u in range(4)]
    load_weights(nc, ctx, "f", units[0:4], rho[:, 0:1], scl[:, 0:1], None, ident16[:, :], None)
    load_weights(nc, ctx, "h", [(a, 0, c) for a, _, c in units[4:8]], rho[:, 1:2], scl[:, 1:2], None,
                 ident16[:, :], None)

    x1 = sb("f_x1", [P, 2, FN, C])
    bn = sb("f_bn", [P, FN, 6])
    mv = sb("f_mv", [P, FN, 2])
    ln_a, ln_r, ln_t, ln_n = (sb(f"f_ln_{c}", [P, FN]) for c in "artn")
    xh = sb("f_xh", [P, FN, C], F16)
    xT = sb("f_xT", [P, G, FT], F16)
    hT = sb("f_hT", [P, NH, FT], F16)
    e16 = sb("f_e16", [P, FN, C], F16)
    o = sb("f_o", [P, FN, C])
    xr = sb("f_xr", [P, FN, C])

    up = ps("up_ps", [P, 4, C])
    down = ps("down_ps", [P, 2, C])
    trp = ps("f_trp", [P, 2, 2 * C], F16)

    s_ld = step("f_ld", 1, 16)
    s_rs = step("f_rs", 1, 16)
    s_st = step("f_st", 1, 16)
    s_bn = step("f_sbn", 2 * FN)
    s_ln = step("f_sln", 2 + RSQRT_STEPS)
    s_xh = step("f_sxh", FN)
    s_tr = step("f_str", 2)
    s_xT = step("f_sxT", 2)
    s_up = step("f_sup", NH)
    s_h = step("f_sh", NH)
    s_dn = step("f_sdn", FN)
    s_e = step("f_se", FN)
    s_o = step("f_so", FN)

    def blk(x, n):
        return x[bass.ds(n * FN, FN), :, :].rearrange("t p c -> p t c")

    def sp_block(eng, n, load):
        s_o.wait_apart(eng, n - 1)
        s_rs.done(eng.dma_start(xr[:, :, :], blk(xio_in, n)))
        if load:
            s_xh.wait_apart(eng, n + 1)
            s_ld.done(eng.dma_start(x1[:, 0, :, :], blk(xio_in, n + 2)))
        s_o.wait_apart(eng, n)
        s_st.done(eng.dma_start(blk(out, n), o[:, :, :]))

    def dve_ln(eng, n):
        s_ld.wait(eng, n)
        for t in range(FN):
            s_bn.done(eng.bn_stats(bn[:, t, :], x1[:, 0, t, :]))
        for t in range(FN):
            s_bn.wait_apart(eng, n, t + 1)
            s_bn.done(eng.bn_aggr(mv[:, t, :], bn[:, t, :]))
        s_bn.wait(eng, n)
        s_ln.done(eng.tensor_scalar(ln_a[:, :], mv[:, :, 1], LN_EPS, None, ALU.add))
        s_ln.wait(eng, n, 1)
        rsqrt(eng, s_ln, n, ln_a[:, :], ln_r[:, :], ln_t[:, :], 1)
        s_ln.done(eng.scalar_tensor_tensor(out=ln_n[:, :], in0=mv[:, :, 0], scalar=-1.0, in1=ln_r[:, :],
                                           op0=ALU.mult, op1=ALU.mult))

    def dve_xT(eng, n):
        s_up.wait(eng, n - 1)
        for k in range(2):
            s_tr.wait(eng, n, k + 1)
            s_xT.done(eng.tensor_copy(xT[:, 2 * k:2 * k + 2, :], trp[:, k, :].rearrange("p (g t) -> p g t", g=2)))

    def dve_block(eng, n, ahead):
        if ahead:
            dve_ln(eng, n + 1)
            dve_xT(eng, n + 1)
        for t in range(FN):
            s_dn.wait(eng, n, t + 1)
            s_o.wait(eng, n - 1, t + 1)
            s_e.done(eng.scalar_tensor_tensor(out=e16[:, t, :], in0=down[:, t % 2, :], scalar=rho[:, 1:2],
                                              in1=b1[:, :], op0=ALU.mult, op1=ALU.add))

    def act_norm(eng, n):
        s_ln.wait(eng, n)
        s_tr.wait(eng, n - 1)
        for t in range(FN):
            s_xh.done(eng.activation(xh[:, t, :], x1[:, 0, t, :], ACT.Identity, bias=ln_n[:, t:t + 1],
                                     scale=ln_r[:, t:t + 1]))

    def act_block(eng, n, ahead):
        s_dn.wait(eng, n - 1)
        for k in range(NH):
            if k == NH // 2 and ahead:
                act_norm(eng, n + 1)
            s_up.wait(eng, n, k + 1)
            s_h.done(eng.activation(hT[:, k, :], up[:, k % 4, :], ACT.Gelu, bias=b0[:, k:k + 1], scale=rho[:, 0:1]))

    def pe_transposes(eng, n):
        s_xh.wait(eng, n)
        for k in range(2):
            s_xT.wait(eng, n - 1, k + 1)
            for gg in range(2):
                for t in range(FN):
                    tr = eng.transpose(trp[:, k, gg * FT + P * t:gg * FT + P * t + P], xh[:, t, rows(2 * k + gg)],
                                       ident16[:, :])
            s_tr.done(tr)

    def pe_block(eng, n, ahead):
        s_xT.wait(eng, n)
        for k in range(NH):
            s_h.wait(eng, n, k - 3) if k >= 4 else s_h.wait(eng, n - 1, NH - 3 + k)
            for kk in range(G):
                for a in range(2):
                    mm = eng.matmul(up[:, k % 4, :], W0T[:, a, kk, rows(k)], xT[:, kk, :],
                                    start=(kk == 0 and a == 0), stop=(kk == G - 1 and a == 1))
            s_up.done(mm)
        if ahead:
            pe_transposes(eng, n + 1)
        for t in range(FN):
            s_e.wait(eng, n, t - 1) if t >= 2 else s_e.wait(eng, n - 1, FN - 1 + t)
            s_h.wait(eng, n)
            for k in range(NH):
                for a in range(2):
                    mm = eng.matmul(down[:, t % 2, :], hT[:, k, rows(t)], W1T[:, a, k, :],
                                    start=(k == 0 and a == 0), stop=(k == NH - 1 and a == 1))
            s_dn.done(mm)

    def pool_block(eng, n, ahead):
        s_rs.wait(eng, n)
        s_st.wait(eng, n - 1)
        for t in range(FN):
            s_e.wait(eng, n, t + 1)
            s_o.done(eng.tensor_tensor(o[:, t, :], e16[:, t, :], xr[:, t, :], ALU.add))

    def every_block(eng, fn):
        fn(eng, 0, True)
        with eng.Fori(1, nb - 1) as n:
            fn(eng, n, True)
        fn(eng, nb - 1, False)

    with nc.Block() as block:
        @block.sync
        def _(eng):
            s_ld.done(eng.dma_start(x1[:, 0, :, :], blk(xio_in, 0)))
            s_xh.wait(eng, 0)
            s_ld.done(eng.dma_start(x1[:, 0, :, :], blk(xio_in, 1)))
            sp_block(eng, 0, True)
            with eng.Fori(1, nb - 2) as n:
                sp_block(eng, n, True)
            sp_block(eng, nb - 2, False)
            sp_block(eng, nb - 1, False)
            s_st.wait(eng, nb - 1)

        @block.vector
        def _(eng):
            f_scale.done(eng.tensor_scalar(rho[:, :], rho[:, :], 1.0 / KS, None, ALU.mult))
            f_scale.wait(eng, 0)
            dve_ln(eng, 0)
            dve_xT(eng, 0)
            every_block(eng, dve_block)

        @block.scalar
        def _(eng):
            f_scale.wait(eng, 0)
            act_norm(eng, 0)
            every_block(eng, act_block)

        @block.tensor
        def _(eng):
            pe_transposes(eng, 0)
            every_block(eng, pe_block)

        @block.gpsimd
        def _(eng):
            every_block(eng, pool_block)


def build(nc, a, consts, x1, out):
    tiles = lambda v: v.rearrange("b (t p) c -> (b t) p c", p=P)
    ntok = a["L0_attn_x"].shape[0] * a["L0_attn_x"].shape[1]
    with ExitStack() as ctx:
        attention(nc, ctx, tiles(a["L0_attn_x"]), x1,
                  [a[f"L0_attn_time_maa_{m}"] for m in "krvg"], [a[f"L0_attn_W{m}"] for m in "krvgo"],
                  a["L0_attn_time_decay"], a["L0_attn_time_faaaa"], a["L0_attn_gamma"], a["L0_attn_beta"],
                  consts, ntok // BT)
    with ExitStack() as ctx:
        ffn(nc, ctx, x1, tiles(out), a["L0_ffn_W0"], a["L0_ffn_bias0"], a["L0_ffn_W1"], a["L0_ffn_bias1"],
            consts, ntok // FT)


_INS = ['L0_attn_x', 'L0_attn_time_maa_k', 'L0_attn_time_maa_v', 'L0_attn_time_maa_r', 'L0_attn_time_maa_g',
        'L0_attn_time_decay', 'L0_attn_time_faaaa', 'L0_attn_Wr', 'L0_attn_Wk', 'L0_attn_Wv', 'L0_attn_Wg',
        'L0_attn_Wo', 'L0_attn_gamma', 'L0_attn_beta', 'L0_ffn_W0', 'L0_ffn_bias0', 'L0_ffn_W1', 'L0_ffn_bias1']


def constants():
    r = np.arange(P)
    i, j = np.arange(Q)[None, :], (r % Q)[:, None]
    same_head = (r[:, None] // N == r[None, :] // N).astype(np.float32)
    return {
        "ident": np.eye(P, dtype=np.float32),
        "ident16": np.eye(P, dtype=np.float16),
        "centring": (np.eye(P) - same_head / N).astype(np.float32),
        "headmask": same_head,
        "dist": np.maximum(i - j - 1, 0).astype(np.float32),
        "after": ((i > j) * ATT_S).astype(np.float32),
        "same": ((i == j) * ATT_S).astype(np.float32),
        "ages": np.stack([-(r % Q), -(Q - 1 - r % Q)], 1).astype(np.float32),
    }


def kernel(**inputs):
    import concourse.bacc as bacc
    from concourse.bass_utils import run_bass_kernel_spmd

    nc = bacc.Bacc("TRN2", target_bir_lowering=False, num_devices=1)
    arrays, aps, consts = {}, {}, {}
    for name in _INS:
        v = np.ascontiguousarray(inputs[name])
        arrays[f"in_{name}"] = v
        aps[name] = nc.dram_tensor(f"in_{name}", v.shape, mybir.dt.from_np(v.dtype), kind="ExternalInput").ap()
    for name, v in constants().items():
        v = np.ascontiguousarray(v)
        arrays[f"const_{name}"] = v
        consts[name] = nc.dram_tensor(f"const_{name}", v.shape, mybir.dt.from_np(v.dtype), kind="ExternalInput").ap()
    shape = inputs["L0_attn_x"].shape
    tiles = shape[0] * shape[1] // P
    x1 = nc.dram_tensor("x1_dram", (tiles, P, C), F32, kind="Internal").ap()
    out = nc.dram_tensor("out", shape, F32, kind="ExternalOutput").ap()
    build(nc, aps, consts, x1, out)
    r = run_bass_kernel_spmd(nc, [arrays], core_ids=[0])
    return r.results[0]["out"]
```

```python
from contextlib import ExitStack

import numpy as np

import concourse.bass as bass
from concourse import mybir

F32, F16, I32 = mybir.dt.float32, mybir.dt.float16, mybir.dt.int32
ALU = mybir.AluOpType
ACT = mybir.ActivationFunctionType
AX = mybir.AxisListType

P = 128
C = 512
H, N = 32, 16
G = C // P
HID = 2048
Q = 64
BT, NT = 256, 2
NCH = BT // Q
T = 2048
FT, FN = 512, 4
LN_EPS = 1e-5
GN_EPS = 1e-5 * 144
KS = 2.0 ** 10
ATT_S = 2.0 ** -5
STATE_S = 2.0 ** -7
YG_S = 2.0 ** -1
EXP_BITS = 0x7F800000
RSQRT_MAGIC = 0x5F3759DF


class Step:

    def __init__(self, nc, ctx, name, per, unit=1, passed=None):
        self.sem = ctx.enter_context(nc.semaphore(name))
        self.per, self.unit = per, unit
        self.passed = passed

    def done(self, instruction):
        return instruction.then_inc(self.sem, self.unit)

    def wait(self, eng, block, k=None):
        value = (block * self.per + (self.per if k is None else k)) * self.unit
        if not isinstance(value, int) or value > 0:
            eng.wait_ge(self.sem, value)

    def wait_apart(self, eng, block, k=None):
        self.wait(eng, block, k)
        if not isinstance(block, int):
            eng.sem_inc(self.passed, 1)


def rsqrt(eng, step, block, x, y, t, first):
    half = dict(scalar=-0.5, in1=x, op0=ALU.mult, op1=ALU.mult)
    newton = [lambda: eng.tensor_tensor(t, y, y, ALU.mult),
              lambda: eng.scalar_tensor_tensor(out=t, in0=t, **half),
              lambda: eng.scalar_tensor_tensor(out=y, in0=t, scalar=1.5, in1=y, op0=ALU.add, op1=ALU.mult)]
    guess = [lambda: eng.tensor_scalar(t.bitcast(I32), x.bitcast(I32), 1, None, ALU.logical_shift_right),
             lambda: eng.tensor_scalar(y.bitcast(I32), t.bitcast(I32), -1.0, float(RSQRT_MAGIC), ALU.mult, ALU.add)]
    for k, instruction in enumerate(guess + 3 * newton):
        step.done(instruction())
        yield
        step.wait(eng, block, first + k + 1)


def in_turn(*parts):
    parts = list(parts)
    while parts:
        parts = [part for part in parts if next(part, parts) is None]


RSQRT_STEPS = 11


def load_weights(nc, ctx, tag, units, rho, scl, centre, ident16, centring, load_first, load_last, s_const):
    nu, nw = len(units), rho.shape[1]
    with ExitStack() as own:
        raw = own.enter_context(nc.sbuf_tensor(f"{tag}raw", [P, nu, G, C], F32))
        nat = own.enter_context(nc.sbuf_tensor(f"{tag}nat", [P, 2, 2, G, C], F16))
        junk = own.enter_context(nc.sbuf_tensor(f"{tag}junk", [P, G * C], F32))
        sums = own.enter_context(nc.sbuf_tensor(f"{tag}sums", [P, nu, G], F32))
        most = own.enter_context(nc.sbuf_tensor(f"{tag}most", [P, nw], F32))
        tps = own.enter_context(nc.psum_tensor(f"{tag}tps", [P, 4, 2 * C], F16))
        cps = own.enter_context(nc.psum_tensor(f"{tag}cps", [P, 4, C], F32))
        landed = [Step(nc, own, f"{tag}landed{u}", 1, 16) for u in range(nu)]
        s_cen = Step(nc, own, f"{tag}cen", 1)
        s_cent = Step(nc, own, f"{tag}cent", 1)
        s_sum = Step(nc, own, f"{tag}sum", 1)
        s_max = Step(nc, own, f"{tag}max", 1)
        s_all = Step(nc, own, f"{tag}all", 1)
        s_norm = Step(nc, own, f"{tag}norm", 1)
        s_scl = Step(nc, own, f"{tag}scl", 1)
        s_hi = Step(nc, own, f"{tag}hi", 1)
        s_lo = Step(nc, own, f"{tag}lo", 1)
        s_tr = Step(nc, own, f"{tag}tr", 4)
        s_evd = Step(nc, own, f"{tag}evd", 2)
        s_eva = Step(nc, own, f"{tag}eva", 2)
        cols = [c for _, c, _ in units]
        by_norm = sorted(range(nu), key=lambda u: u == centre)

        def evacuate(eng, u, hl, step):
            dst = units[u][2]
            for half in range(2):
                s_tr.wait(eng, u, 2 * hl + half + 1)
                out, src = dst[:, hl, 2 * half:2 * half + 2, :], tps[:, 2 * hl + half, :].rearrange(
                    "p (k c) -> p k c", k=2)
                step.done(eng.activation(out, src, ACT.Copy) if hl else eng.tensor_copy(out, src))

        with nc.Block() as block:

            @block.sync
            def _(eng):
                load_first(eng)
                for u in sorted(range(nu), key=lambda u: u != centre):
                    src = units[u][0]
                    landed[u].done(eng.dma_start(raw[:, u, :, :], src.rearrange("(b p) c -> p b c", p=P)))
                load_last(eng)

            @block.scalar
            def _(eng):
                for i, u in enumerate(by_norm):
                    landed[u].wait(eng, 0)
                    if u == centre:
                        s_cent.wait(eng, 0)
                    for b in range(G):
                        k = i * G + b
                        s_sum.wait(eng, k - 1)
                        s_sum.done(eng.activation(junk[:, 0:C], raw[:, u, b, :], ACT.Square,
                                                  accum_out=sums[:, u, b:b + 1]))
                s_all.wait(eng, 0)
                s_norm.done(eng.activation(rho, most[:, :], ACT.Sqrt))
                for u in range(nu):
                    s_scl.wait(eng, 3)
                    s_tr.wait(eng, u - 2)
                    s_hi.done(eng.activation(nat[:, u % 2, 0, :, :], raw[:, u, :, :], ACT.Identity,
                                             scale=scl[:, cols[u]:cols[u] + 1]))
                    if u:
                        evacuate(eng, u - 1, 1, s_eva)
                evacuate(eng, nu - 1, 1, s_eva)

            @block.gpsimd
            def _(eng):
                s_max.wait(eng, nw - 1)
                s_all.done(eng.partition_all_reduce(most[:, :], most[:, :], P, bass.bass_isa.ReduceOp.max))

            @block.vector
            def _(eng):
                if centre is not None:
                    s_cen.wait(eng, 0)
                    s_cent.done(eng.tensor_copy(raw[:, centre, :, :], cps[:, :, :]))
                for w in sorted(range(nw), key=lambda w: centre is not None and w == cols[centre]):
                    us = [u for u in range(nu) if cols[u] == w]
                    s_sum.wait(eng, by_norm.index(us[-1]) * G + G - 1)
                    s_max.done(eng.tensor_reduce(most[:, w:w + 1], sums[:, us[0]:us[-1] + 1, :], AX.XY, ALU.max))
                s_norm.wait(eng, 0)
                s_scl.done(eng.tensor_scalar(rho, rho, 1e-12, None, ALU.max))
                s_scl.wait(eng, 0)
                s_scl.done(eng.tensor_scalar(rho.bitcast(I32), rho.bitcast(I32), EXP_BITS, None, ALU.bitwise_and))
                s_scl.wait(eng, 1)
                s_scl.done(eng.reciprocal(scl, rho))
                s_scl.wait(eng, 2)
                s_scl.done(eng.tensor_scalar(scl, scl, KS, None, ALU.mult))
                for u in range(nu):
                    s_scl.wait(eng, 3)
                    s_hi.wait(eng, u)
                    s_lo.done(eng.scalar_tensor_tensor(
                        out=nat[:, u % 2, 1, :, :].rearrange("p b c -> p (b c)"),
                        in0=raw[:, u, :, :].rearrange("p b c -> p (b c)"),
                        scalar=scl[:, cols[u]:cols[u] + 1],
                        in1=nat[:, u % 2, 0, :, :].rearrange("p b c -> p (b c)"),
                        op0=ALU.mult, op1=ALU.subtract))
                    if u:
                        evacuate(eng, u - 1, 0, s_evd)
                evacuate(eng, nu - 1, 0, s_evd)

            @block.tensor
            def _(eng):
                s_const.wait(eng, 1)
                if centre is not None:
                    landed[centre].wait(eng, 0)
                    for b in range(G):
                        mm = eng.matmul(cps[:, b, :], centring, raw[:, centre, b, :], start=True, stop=True)
                    s_cen.done(mm)
                for u in range(nu):
                    for hl in range(2):
                        (s_lo if hl else s_hi).wait(eng, u)
                        for half in range(2):
                            (s_eva if hl else s_evd).wait(eng, u - 1, half + 1)
                            for kk in range(2):
                                for b in range(G):
                                    k = 2 * half + kk
                                    tr = eng.transpose(tps[:, 2 * hl + half, kk * C + b * P:kk * C + (b + 1) * P],
                                                       nat[:, u % 2, hl, b, k * P:(k + 1) * P], ident16)
                            s_tr.done(tr)


def attention(nc, ctx, x, x1_out, maas, weights, decay, bonus, gamma, beta, consts, nb):

    def sb(name, shape, dt=F32):
        return ctx.enter_context(nc.sbuf_tensor(name, shape, dt))

    def ps(name, shape, dt=F32):
        return ctx.enter_context(nc.psum_tensor(name, shape, dt))

    s_passed = ctx.enter_context(nc.semaphore("a_passed"))

    def step(name, per, unit=1):
        return Step(nc, ctx, name, per, unit, s_passed)

    ident = sb("ident", [P, P])
    ident16 = sb("ident16", [P, P], F16)
    centring = sb("centring", [P, P])
    WT = sb("WT", [P, 5, 2, G, C], F16)
    rho = sb("rho", [P, 5])
    scl = sb("scl", [P, 5])
    maa = sb("maa", [P, 4, G])
    wmask = sb("wmask", [P, NT * 8, Q])
    headmask = sb("headmask", [P, P])
    wb = sb("wb", [P, H])
    wk = sb("wk", [P, H])
    ws = sb("ws", [P, G])
    wsf = sb("wsf", [P, G])
    flag = sb("flag", [P, nb + 1])
    gam = sb("gam", [P, G])
    bet = sb("bet", [P, G])
    gn_eps = sb("gn_eps", [P, 1])
    half_rho_g = sb("half_rho_g", [P, 1])
    out_scale = sb("out_scale", [P, 1])
    s_const = step("s_const", 1, 16)

    K_, R_, V_, G_, O_ = range(5)

    with ExitStack() as own:
        def tb(name, shape):
            return own.enter_context(nc.sbuf_tensor(name, shape, F32))
        dist = tb("dist", [P, Q])
        after = tb("after", [P, Q])
        same = tb("same", [P, Q])
        ages = tb("ages", [P, 2])
        ep = tb("ep", [P, NT * 8])
        up = tb("up", [P, NT * 8])
        un = tb("un", [P, H])
        en = tb("en", [P, H])
        ec = tb("ec", [P, G])
        diag = tb("diag", [P, NT * 8, Q])
        s_in = Step(nc, own, "t_in", 1, 16)
        s_e = Step(nc, own, "t_e", 1)
        s_n = Step(nc, own, "t_n", 1)
        s_x = Step(nc, own, "t_x", 1)
        s_t = Step(nc, own, "t_t", 1)
        loads = [(dist[:, :], consts["dist"]), (after[:, :], consts["after"]), (same[:, :], consts["same"]),
                 (ages[:, :], consts["ages"]),
                 (ident[:, :], consts["ident"]), (headmask[:, :], consts["headmask"]),
                 (en[:, :], decay.rearrange("h o -> (h o)").partition_broadcast(P)),
                 (un[:, :], bonus.rearrange("h o -> (h o)").partition_broadcast(P)),
                 (gam[:, :], gamma.rearrange("(g p) -> p g", p=P)), (bet[:, :], beta.rearrange("(g p) -> p g", p=P))]
        for h in range(8):
            loads.append((ec[N * h:N * h + N, :],
                          decay.rearrange("(g h) o -> h (g o)", h=8)[h].partition_broadcast(N)))
        for m, v in enumerate(maas):
            loads.append((maa[:, m, :], v.rearrange("a b (g p) -> p (a b g)", p=P)))

        def load_first(eng):
            s_const.done(eng.dma_start(centring[:, :], consts["centring"]))
            s_const.done(eng.dma_start(ident16[:, :], consts["ident16"]))

        def load_last(eng):
            for dst, src in loads:
                s_in.done(eng.dma_start(dst, src, allow_slow_non_contiguous=True))
            s_in.wait(eng, len(loads) - 1)

        load_weights(nc, ctx, "a", [(weights[w], w, WT[:, w, :, :, :]) for w in range(5)],
                     rho[:, :], scl[:, :], V_, ident16[:, :], centring[:, :], load_first, load_last, s_const)

        with nc.Block() as block:

            @block.scalar
            def _(eng):
                for t in (en, ec):
                    s_e.done(eng.activation(t[:, :], t[:, :], ACT.Exp))
                s_n.wait(eng, 5)
                for q in range(NT * 8):
                    s_x.done(eng.activation(wmask[:, q, :], dist[:, :], ACT.Exp, scale=ep[:, q:q + 1]))
                s_x.done(eng.activation(wb[:, :], wb[:, :], ACT.Exp))
                s_x.done(eng.activation(wk[:, :], wk[:, :], ACT.Exp))
                s_x.done(eng.activation(ws[:, :], ec[:, :], ACT.Exp, scale=-float(Q)))

            @block.vector
            def _(eng):
                nq = NT * 8
                s_e.wait(eng, 1)
                s_n.done(eng.tensor_scalar(wb[:, :], en[:, :], ages[:, 0:1], None, ALU.mult))
                s_n.done(eng.tensor_scalar(wk[:, :], en[:, :], ages[:, 1:2], None, ALU.mult))
                for p in range(2):
                    half = slice(Q * p, Q * p + Q)
                    s_n.done(eng.tensor_scalar(ep[half, :], en[half, p:H:2], -1.0, None, ALU.mult))
                    s_n.done(eng.tensor_copy(up[half, :], un[half, p:H:2]))
                s_n.wait(eng, 5)
                s_n.done(eng.tensor_tensor(diag[:, :, :], same[:, :].unsqueeze(1).to_broadcast([P, nq, Q]),
                                           up[:, :].unsqueeze(2).to_broadcast([P, nq, Q]), ALU.mult))
                s_x.wait(eng, nq + 2)
                s_t.done(eng.tensor_tensor(wmask[:, :, :], wmask[:, :, :],
                                           after[:, :].unsqueeze(1).to_broadcast([P, nq, Q]), ALU.mult))
                s_t.wait(eng, 0)
                s_n.wait(eng, 6)
                s_t.done(eng.tensor_tensor(wmask[:, :, :], wmask[:, :, :], diag[:, :, :], ALU.add))
                s_t.done(eng.tensor_scalar(wb[:, :], wb[:, :], ATT_S / STATE_S, None, ALU.mult))
                s_t.done(eng.tensor_scalar(wk[:, :], wk[:, :], STATE_S / KS, None, ALU.mult))
                s_t.done(eng.tensor_scalar(gam[:, :], gam[:, :], YG_S / (2 * KS), None, ALU.mult))
                s_t.done(eng.tensor_scalar(bet[:, :], bet[:, :], YG_S / (2 * KS), None, ALU.mult))
                s_t.done(eng.memset(flag[:, :], 1.0))
                s_t.wait(eng, 6)
                s_t.done(eng.memset(flag[:, 0:nb + 1:T // BT], 0.0))
                s_t.done(eng.tensor_tensor(gn_eps[:, :], rho[:, K_:K_ + 1], rho[:, R_:R_ + 1], ALU.mult))
                s_t.wait(eng, 8)
                s_t.done(eng.tensor_tensor(gn_eps[:, :], gn_eps[:, :], rho[:, V_:V_ + 1], ALU.mult))
                s_t.wait(eng, 9)
                s_t.done(eng.reciprocal(gn_eps[:, :], gn_eps[:, :]))
                s_t.wait(eng, 10)
                s_t.done(eng.tensor_tensor(gn_eps[:, :], gn_eps[:, :], gn_eps[:, :], ALU.mult))
                s_t.wait(eng, 11)
                s_t.done(eng.tensor_scalar(gn_eps[:, :], gn_eps[:, :], GN_EPS * ATT_S ** 2, None, ALU.mult))
                s_t.done(eng.tensor_scalar(half_rho_g[:, :], rho[:, G_:G_ + 1], 0.5 / KS, None, ALU.mult))
                s_t.done(eng.tensor_tensor(out_scale[:, :], rho[:, G_:G_ + 1], rho[:, O_:O_ + 1], ALU.mult))
                s_t.wait(eng, 14)
                s_t.done(eng.tensor_scalar(out_scale[:, :], out_scale[:, :], 1.0 / (KS * YG_S), None, ALU.mult))

    xa = sb("xa", [P, NT, C])
    bn = sb("bn", [P, NT, 6])
    mv = sb("mv", [P, NT, 2])
    ln_a, ln_r, ln_t, ln_n = (sb(f"ln_{c}", [P, NT]) for c in "artn")
    xnT = sb("xnT", [P, G, BT + 1])
    dx = sb("dx", [P, G, BT])
    mixf = sb("mixf", [P, 2, G, BT])
    mix = sb("mix", [P, 4, 2, G, BT], F16)
    kT = sb("kT", [P, 2, G, BT], F16)
    rT = sb("rT", [P, 2, G, BT], F16)
    kx = sb("kx", [P, 2 * G, NCH, 2, Q], F16)
    rx = sb("rx", [P, 2, G, 4, BT], F16)
    kN = sb("kN", [P, NT, 2, C], F16)
    vN = sb("vN", [P, NT, 2, 2, C // 2], F16)
    vw32 = sb("vw32", [P, NT, C])
    vw = sb("vw", [P, NT, 2, C], F16)
    vbd = sb("vbd", [P, NT, 2, 2, 2, C // 2], F16)
    tg = sb("tg", [P, NT, C])
    gT = sb("gT", [P, G, BT])
    att32 = sb("att32", [P, 2, C])
    att = sb("att", [P, 2, 2, 2 * C], F16)
    kv = sb("kv", [P, C])
    S = sb("S", [P, C])
    Sw = sb("Sw", [P, C])
    Shl = sb("Shl", [P, 2, 2, C], F16)
    yi = sb("yi", [P, C])
    y = sb("y", [P, NT, C])
    ysq = sb("ysq", [P, C])
    gn_s, gn_a, gn_r, gn_t = (sb(f"gn_{c}", [P, NT, H]) for c in "sart")
    ygT = sb("ygT", [P, G, BT])
    yg = sb("yg", [P, 2, G, BT], F16)
    x1 = sb("x1", [P, NT, C])

    big = ps("big", [P, 2, C])
    sc = ps("sc", [P, 2, C])
    Y = ps("Y", [P, 2, C])
    kvp = ps("kvp", [P, C])
    trp = ps("trp", [P, 2 * C], F16)

    s_xa = step("s_xa", 1, 16)
    s_xr = step("s_xr", 1, 16)
    s_st = step("s_st", 1, 16)
    s_kx = step("s_kx", 8, 16)
    s_rx = step("s_rx", 4, 16)
    s_vbd = [step(f"s_vbd{t}", 4, 16) for t in range(NT)]
    s_bn = step("s_bn", 4)
    s_ln = step("s_ln", 2 + RSQRT_STEPS)
    s_xn = step("s_xn", NT)
    s_X = step("s_X", NT)
    s_xT = step("s_xT", NT)
    s_carry = step("s_carry", 1)
    s_dx = step("s_dx", 1)
    s_mix = step("s_mix", 4)
    s_mh = step("s_mh", 4)
    s_ml = step("s_ml", 4)
    s_pK = step("s_pK", 2)
    s_pR = step("s_pR", 2)
    s_pG = step("s_pG", 2)
    s_pV = step("s_pV", NT)
    s_kh = step("s_kh", 2)
    s_kl = step("s_kl", 2)
    s_rh = step("s_rh", 2)
    s_rl = step("s_rl", 2)
    s_vh = step("s_vh", NT)
    s_vl = step("s_vl", NT)
    s_vw = step("s_vw", NT)
    s_vwh = step("s_vwh", NT)
    s_vwl = step("s_vwl", NT)
    s_kt = step("s_kt", NT)
    s_kN = step("s_kN", NT)
    s_tg = step("s_tg", 2)
    s_gT = step("s_gT", 2)
    s_sc = step("s_sc", 2 * NCH)
    s_am = step("s_am", 2 * NCH)
    s_ah = step("s_ah", 2 * NCH)
    s_al = step("s_al", 2 * NCH)
    s_av = step("s_av", NCH)
    s_in = step("s_in", NCH)
    s_kv = step("s_kv", NCH)
    s_km = step("s_km", NCH)
    s_S = step("s_S", NCH)
    s_wsf = step("s_wsf", 1)
    s_Sh = step("s_Sh", NCH)
    s_Sl = step("s_Sl", NCH)
    s_Sw = step("s_Sw", NCH)
    s_yi = step("s_yi", NT)
    s_y = step("s_y", NT)
    s_sq = step("s_sq", NT)
    s_gs = step("s_gs", NT)
    s_gn = step("s_gn", 1 + RSQRT_STEPS)
    s_yn = step("s_yn", NT)
    s_yT = step("s_yT", NT)
    s_af = step("s_af", G)
    s_yg = step("s_yg", NT)
    s_ygh = step("s_ygh", NT)
    s_ygl = step("s_ygl", NT)
    s_Wo = step("s_Wo", NT)
    s_x1 = step("s_x1", NT)
    s_zero = step("s_zero", 1)

    PASSES = ((0, 0), (0, 1), (1, 0))
    def rows(t):
        return slice(P * t, P * t + P)


    def pe_project_T(eng, out, w, m, half):
        for gg in range(2):
            g = 2 * half + gg
            for i, (a, b) in enumerate(PASSES):
                for kk in range(G):
                    mm = eng.matmul(out[:, gg * BT:(gg + 1) * BT], WT[:, w, a, kk, rows(g)],
                                    mix[:, m, b, kk, :], start=(i == 0 and kk == 0), stop=(i == 2 and kk == G - 1))
        return mm

    def pe_X(eng, n, t):
        s_xn.wait(eng, n, t + 1)
        for g in range(G):
            tr = eng.transpose(big[:, t, rows(g)], xa[:, t, rows(g)], ident[:, :])
        s_X.done(tr)

    def pe_tail_yT(eng, n):
        for t in range(NT):
            s_yn.wait(eng, n, t + 1)
            for g in range(G):
                tr = eng.transpose(big[:, t, rows(g)], y[:, t, rows(g)], ident[:, :])
            s_yT.done(tr)

    def pe_tail_Wo(eng, n, t):
        s_ygl.wait(eng, n, t + 1)
        for i, (a, b) in enumerate(PASSES):
            for kk in range(G):
                mm = eng.matmul(big[:, t, :], yg[:, a, kk, rows(t)], WT[:, 4, b, kk, :],
                                start=(i == 0 and kk == 0), stop=(i == 2 and kk == G - 1))
        s_Wo.done(mm)

    def pe_block(eng, n, tail, ahead):
        def mixed(m):
            s_ml.wait(eng, n, m + 1)
            s_mh.wait(eng, n, m + 1)

        mixed(0)
        for half in range(2):
            s_am.wait(eng, n - 1, 2 * NCH - 1 + half)
            s_pK.done(pe_project_T(eng, sc[:, half, :], 0, 0, half))
        mixed(1)
        s_km.wait(eng, n - 1)
        for half in range(2):
            s_pR.done(pe_project_T(eng, big[:, half, :], 1, 1, half))

        def k_tokens(t):
            s_kN.wait(eng, n - 1) if t == 0 else s_kN.wait(eng, n, 1)
            s_kl.wait(eng, n)
            for hl in range(2):
                for g in range(G):
                    tr = eng.transpose(trp[:, hl * C + g * P:hl * C + (g + 1) * P], kT[:, hl, g, rows(t)],
                                       ident16[:, :])
            s_kt.done(tr)

        mixed(2)
        for t in range(NT):
            if t:
                k_tokens(0)
            (s_yi if t else s_y).wait(eng, n - 1)
            for i, (a, b) in enumerate(PASSES):
                for kk in range(G):
                    mm = eng.matmul(Y[:, t, :], mix[:, 2, a, kk, rows(t)], WT[:, 2, b, kk, :],
                                    start=(i == 0 and kk == 0), stop=(i == 2 and kk == G - 1))
            s_pV.done(mm)
            if t == 0:
                s_rl.wait(eng, n)
                if tail:
                    pe_tail_yT(eng, n - 1)
        k_tokens(1)
        if ahead:
            for t in range(NT):
                if tail and t == 0:
                    s_af.wait(eng, n - 1)
                pe_X(eng, n + 1, t)
        elif tail:
            s_af.wait(eng, n - 1)

        def scores(c):
            if c == 0:
                s_kx.wait(eng, n)
                s_rx.wait(eng, n)
                s_kl.wait(eng, n)
            for x in range(2):
                s_am.wait(eng, n, 2 * (c - 1) + x + 1) if c else None
                for gg in range(2):
                    g = 2 * x + gg
                    for i, (a, b) in enumerate(PASSES):
                        mm = eng.matmul(sc[:, x, gg * BT:(gg + 1) * BT], kx[:, G * a + g, c, :, :].rearrange("p a j -> p (a j)"),
                                        rx[:, b, g, :, Q * c:Q * c + Q], start=(i == 0), stop=(i == 2))
                s_sc.done(mm)

        def att_v(c):
            t, cc = c // 2, c % 2
            out = Y[Q * cc:Q * cc + Q, 0, :]
            if cc == 0:
                s_y.wait(eng, n, t) if t else s_vl.wait(eng, n, 1)
                s_vbd[t].wait(eng, n)
            s_al.wait(eng, n, 2 * c + 2)
            for q in range(16):
                for i, (a, b) in enumerate(PASSES):
                    mm = eng.matmul(out[:, 2 * N * q:2 * N * (q + 1)], att[:, cc, a, Q * q:Q * q + Q],
                                    vbd[:, t, cc, b, :, N * q:N * q + N],
                                    start=(i == 0), stop=(i == 2))
            s_av.done(mm)

        def from_state(c):
            t, cc = c // 2, c % 2
            if cc == 0:
                s_yi.wait(eng, n, t) if t else s_vl.wait(eng, n, 2)
            s_Sl.wait(eng, n, c) if c else s_Sl.wait(eng, n - 1)
            for g in range(G):
                for i, (a, b) in enumerate(PASSES):
                    mm = eng.matmul(Y[Q * cc:Q * cc + Q, 1, rows(g)], rT[:, a, g, Q * c:Q * c + Q],
                                    Shl[:, cc, b, rows(g)], start=(i == 0), stop=(i == 2))
            s_in.done(mm)

        def kv_sum(c):
            t, cc = c // 2, c % 2
            s_km.wait(eng, n, c) if c else s_km.wait(eng, n - 1)
            if cc == 0:
                s_vwl.wait(eng, n, t + 1)
                s_vwh.wait(eng, n, t + 1)
                s_kN.wait(eng, n, t + 1)
            part = slice(Q * cc, Q * cc + Q)
            for g in range(G):
                for i, (a, b) in enumerate(PASSES):
                    mm = eng.matmul(kvp[:, rows(g)], kN[part, t, a, rows(g)], vw[part, t, b, rows(g)],
                                    start=(i == 0), stop=(i == 2))
            s_kv.done(mm)

        def gate(half):
            if half == 0:
                mixed(3)
            if ahead:
                s_xT.wait(eng, n + 1, half + 1)
            s_pG.done(pe_project_T(eng, big[:, half, :], 3, 3, half))

        def out_tile(t):
            if tail:
                s_gT.wait(eng, n, t + 1)
                pe_tail_Wo(eng, n - 1, t)

        scores(0)
        kv_sum(0)
        gate(0)
        scores(1)
        att_v(0)
        from_state(0)
        gate(1)
        kv_sum(1)
        scores(2)
        att_v(1)
        from_state(1)
        out_tile(0)
        kv_sum(2)
        scores(3)
        att_v(2)
        from_state(2)
        out_tile(1)
        kv_sum(3)
        att_v(3)
        from_state(3)

    def dve_ln(eng, n):
        s_xa.wait(eng, n)
        for t in range(NT):
            s_bn.done(eng.bn_stats(bn[:, t, :], xa[:, t, :]))
            yield
        for t in range(NT):
            s_bn.wait_apart(eng, n, t + 1)
            s_bn.done(eng.bn_aggr(mv[:, t, :], bn[:, t, :]))
            yield
        s_bn.wait(eng, n)
        s_ln.done(eng.tensor_scalar(ln_a[:, :], mv[:, :, 1], LN_EPS, None, ALU.add))
        yield
        s_ln.wait(eng, n, 1)
        yield from rsqrt(eng, s_ln, n, ln_a[:, :], ln_r[:, :], ln_t[:, :], 1)
        s_ln.done(eng.scalar_tensor_tensor(out=ln_n[:, :], in0=mv[:, :, 0], scalar=-1.0, in1=ln_r[:, :],
                                           op0=ALU.mult, op1=ALU.mult))

    def dve_dx(eng, n):
        s_xT.wait(eng, n)
        s_carry.wait(eng, n)
        s_dx.done(eng.tensor_tensor(dx[:, :, :], xnT[:, :, 0:BT], xnT[:, :, 1:BT + 1], ALU.subtract))

    def dve_carry(eng, n):
        s_mix.wait(eng, n - 1)
        s_carry.done(eng.tensor_scalar(xnT[:, :, 0:1], xnT[:, :, BT:BT + 1], flag[:, bass.ds(n, 1)],
                                       None, ALU.mult))

    def dve_mix(eng, n, m):
        if m == 0:
            s_dx.wait(eng, n)
        s_ml.wait(eng, n, m - 1) if m >= 2 else s_ml.wait(eng, n - 1, m + 3)
        for g in range(G):
            last = eng.scalar_tensor_tensor(out=mixf[:, m % 2, g, :], in0=dx[:, g, :], scalar=maa[:, m, g:g + 1],
                                            in1=xnT[:, g, 1:BT + 1], op0=ALU.mult, op1=ALU.add)
            if g == G - 1:
                s_mix.done(last)
            yield

    def dve_lo(eng, projected, dst, half):
        g2 = slice(2 * half, 2 * half + 2)
        return eng.scalar_tensor_tensor(out=dst[:, 1, g2, :], in0=projected.rearrange("p (g t) -> p g t", g=2),
                                        scalar=1.0 / KS, in1=dst[:, 0, g2, :], op0=ALU.mult, op1=ALU.subtract)

    def dve_gated(eng, n):
        s_af.wait(eng, n)
        for t in range(NT):
            s_yg.done(eng.tensor_tensor(ygT[:, :, rows(t)], ygT[:, :, rows(t)], gT[:, :, rows(t)], ALU.mult))

    def dve_residual(eng, n, t):
        s_xr.wait(eng, n)
        s_Wo.wait(eng, n, t + 1)
        s_x1.done(eng.scalar_tensor_tensor(out=x1[:, t, :], in0=big[:, t, :], scalar=out_scale[:, 0:1],
                                           in1=x1[:, t, :], op0=ALU.mult, op1=ALU.add))

    def dve_variance(eng, n, t):
        s_sq.wait(eng, n, t + 1)
        s_gs.done(eng.tensor_reduce(gn_s[:, t, :], ysq[:, :].rearrange("p (h d) -> p h d", h=H), AX.X, ALU.add))

    def dve_normalize(eng, n):
        dve_variance(eng, n, 1)
        yield
        s_gs.wait(eng, n)
        s_gn.done(eng.tensor_scalar(gn_a[:, :, :], gn_s[:, :, :], 1.0 / N, gn_eps[:, 0:1], ALU.mult, ALU.add))
        yield
        s_gn.wait(eng, n, 1)
        yield from rsqrt(eng, s_gn, n, gn_a[:, :, :], gn_r[:, :, :], gn_t[:, :, :], 1)
        for t in range(NT):
            s_yn.done(eng.tensor_tensor(y[:, t, :].rearrange("p (h d) -> p h d", h=H),
                                        y[:, t, :].rearrange("p (h d) -> p h d", h=H),
                                        gn_r[:, t, :].unsqueeze(2).to_broadcast([P, H, N]), ALU.mult))
            yield

    def dve_block(eng, n, tail, ahead):
        def mix_and_k():
            yield from dve_mix(eng, n, 2)
            for half in range(2):
                yield
                yield
                s_kh.wait(eng, n, half + 1)
                s_kl.done(dve_lo(eng, sc[:, half, :], kT, half))
            yield from dve_mix(eng, n, 3)

        chains = [mix_and_k()]
        if tail:
            chains.append(dve_normalize(eng, n - 1))
        if ahead:
            chains.insert(0, dve_ln(eng, n + 1))
        in_turn(*chains)
        def weigh(c):
            for x in range(2):
                s_sc.wait(eng, n, 2 * c + x + 1)
                s_al.wait(eng, n, 2 * c - 1 + x) if c else s_al.wait(eng, n - 1, 2 * NCH - 1 + x)
                s_am.done(eng.tensor_tensor(att32[:, x, :], sc[:, x, :],
                                            wmask[:, 8 * x:8 * x + 8, :].rearrange("p q i -> p (q i)"), ALU.mult))

        for half in range(2):
            s_rh.wait(eng, n, half + 1)
            s_rl.done(dve_lo(eng, big[:, half, :], rT, half))
        for t in range(NT):
            s_pV.wait(eng, n, t + 1)
            s_vw.done(eng.tensor_tensor(vw32[:, t, :].rearrange("p (h d) -> p h d", h=H),
                                        Y[:, t, :].rearrange("p (h d) -> p h d", h=H),
                                        wk[:, :].unsqueeze(2).to_broadcast([P, H, N]), ALU.mult))
            if t:
                weigh(0)
            else:
                if ahead:
                    dve_carry(eng, n + 1)
                s_Sw.wait(eng, n - 1)
                s_wsf.done(eng.tensor_scalar(wsf[:, :], ws[:, :], flag[:, bass.ds(n + 1, 1)], None, ALU.mult))
                if tail:
                    dve_gated(eng, n - 1)
            s_vh.wait(eng, n, t + 1)
            for p in range(2):
                last = eng.scalar_tensor_tensor(
                    out=vN[:, t, 1, p, :].rearrange("p (q d) -> p q d", d=N),
                    in0=Y[:, t, :].rearrange("p (q a d) -> p a q d", a=2, d=N)[:, p], scalar=1.0 / KS,
                    in1=vN[:, t, 0, p, :].rearrange("p (q d) -> p q d", d=N), op0=ALU.mult, op1=ALU.subtract)
            s_vl.done(last)

        def weights_lo(c):
            for x in range(2):
                s_ah.wait(eng, n, 2 * c + x + 1)
                s_al.done(eng.tensor_tensor(att[:, c % 2, 1, C * x:C * x + C], att32[:, x, :],
                                            att[:, c % 2, 0, C * x:C * x + C], ALU.subtract))

        def state(c):
            s_kv.wait(eng, n, c + 1)
            out, src = (b[:, :].rearrange("p (g c) -> p g c", g=G) for b in (kv, kvp))
            mask = headmask[:, :].unsqueeze(1).to_broadcast([P, G, P])
            if c < NCH - 1:
                s_km.done(eng.tensor_tensor(out, src, mask, ALU.mult))
            else:
                s_km.done(eng.scalar_tensor_tensor(out=out, in0=src, scalar=flag[:, bass.ds(n + 1, 1)], in1=mask,
                                                   op0=ALU.mult, op1=ALU.mult))
            s_km.wait(eng, n, c + 1)
            s_Sw.wait(eng, n, c) if c else s_Sw.wait(eng, n - 1)
            s_Sl.wait(eng, n, c) if c else s_Sl.wait(eng, n - 1)
            s_S.done(eng.tensor_tensor(S[:, :], kv[:, :], Sw[:, :], ALU.add))

        def gate(half):
            s_tg.wait(eng, n, half + 1)
            g2 = slice(2 * half, 2 * half + 2)
            s_gT.done(eng.scalar_tensor_tensor(out=gT[:, g2, :], in0=tg[:, half, :].rearrange("p (g t) -> p g t", g=2),
                                               scalar=1.0, in1=big[:, half, :].rearrange("p (g t) -> p g t", g=2),
                                               op0=ALU.add, op1=ALU.mult))

        def take_y(t):
            s_in.wait(eng, n, 2 * t + 2)
            s_av.wait(eng, n, 2 * t + 2)
            s_yi.done(eng.tensor_tensor(yi[:, :].rearrange("p (h d) -> p h d", h=H),
                                        Y[:, 1, :].rearrange("p (h d) -> p h d", h=H),
                                        wb[:, :].unsqueeze(2).to_broadcast([P, H, N]), ALU.mult))
            s_yi.wait(eng, n, t + 1)
            s_yT.wait(eng, n - 1)
            s_y.done(eng.tensor_tensor(y[:, t, :], Y[:, 0, :], yi[:, :], ALU.add))

        if ahead:
            dve_dx(eng, n + 1)
        weights_lo(0)
        if ahead:
            in_turn(dve_mix(eng, n + 1, 0))
        state(0)
        weigh(1)
        gate(0)
        weights_lo(1)
        if ahead:
            in_turn(dve_mix(eng, n + 1, 1))
        state(1)
        weigh(2)
        gate(1)
        weights_lo(2)
        take_y(0)
        if tail:
            dve_residual(eng, n - 1, 0)
        state(2)
        weigh(3)
        dve_variance(eng, n, 0)
        weights_lo(3)
        if tail:
            dve_residual(eng, n - 1, 1)
        state(3)
        take_y(1)

    def act_norm(eng, n):
        s_ln.wait(eng, n)
        for t in range(NT):
            s_xn.done(eng.activation(xa[:, t, :], xa[:, t, :], ACT.Identity, bias=ln_n[:, t:t + 1],
                                     scale=ln_r[:, t:t + 1]))

    def act_xT(eng, n):
        s_dx.wait(eng, n - 1)
        s_mix.wait(eng, n - 1)
        s_carry.wait(eng, n)
        for t in range(NT):
            s_X.wait(eng, n, t + 1)
            s_xT.done(eng.activation(xnT[:, :, 1 + P * t:1 + P * t + P],
                                     big[:, t, :].rearrange("p (g t) -> p g t", g=G), ACT.Copy))

    def act_mix_hi(eng, n, m):
        s_mix.wait(eng, n, m + 1)
        (s_pK, s_pR, s_pV, s_pG)[m].wait(eng, n - 1)
        s_mh.done(eng.activation(mix[:, m, 0, :, :], mixf[:, m % 2, :, :], ACT.Copy))

    def act_gated(eng, n):
        s_yT.wait(eng, n)
        for g in range(G):
            s_af.done(eng.activation(ygT[:, g, :].rearrange("p (t i) -> p t i", t=NT), big[:, :, rows(g)],
                                     ACT.Identity, bias=bet[:, g:g + 1], scale=gam[:, g:g + 1]))

    def act_gated_hi(eng, n):
        for t in range(NT):
            s_yg.wait(eng, n, t + 1)
            s_ygh.done(eng.activation(yg[:, 0, :, rows(t)], ygT[:, :, rows(t)], ACT.Copy))

    def act_block(eng, n, tail, ahead):
        def project_hi(projected, done, dst, half, src):
            projected.wait(eng, n, half + 1)
            done.done(eng.activation(dst[:, 0, 2 * half:2 * half + 2, :],
                                     src[:, half, :].rearrange("p (g t) -> p g t", g=2), ACT.Copy, scale=1.0 / KS))

        def k_tokens(t):
            s_kt.wait(eng, n, t + 1)
            s_kv.wait(eng, n - 1)
            s_kN.done(eng.activation(kN[:, t, :, :], trp[:, :].rearrange("p (a c) -> p a c", a=2), ACT.Copy))

        def v_hi(t):
            s_vbd[t].wait(eng, n - 1)
            s_vw.wait(eng, n, t + 1)
            s_vh.done(eng.activation(vN[:, t, 0, :, :].rearrange("p a (q d) -> p a q d", d=N),
                                     Y[:, t, :].rearrange("p (q a d) -> p a q d", a=2, d=N), ACT.Copy,
                                     scale=1.0 / KS))

        def vw_hi(t):
            s_kv.wait(eng, n - 1)
            s_vwh.done(eng.activation(vw[:, t, 0, :], vw32[:, t, :], ACT.Copy))

        s_kx.wait(eng, n - 1)
        s_kt.wait(eng, n - 1)
        for half in range(2):
            project_hi(s_pK, s_kh, kT, half, sc)
        act_mix_hi(eng, n, 2)
        s_rx.wait(eng, n - 1)
        s_in.wait(eng, n - 1)
        for half in range(2):
            project_hi(s_pR, s_rh, rT, half, big)
        act_mix_hi(eng, n, 3)
        if ahead:
            act_norm(eng, n + 1)
        if tail:
            s_ml.wait(eng, n, 1)
            act_gated(eng, n - 1)
        k_tokens(0)
        v_hi(0)
        vw_hi(0)
        if ahead:
            act_xT(eng, n + 1)
        v_hi(1)
        vw_hi(1)
        def weights_hi(c):
            s_av.wait(eng, n, c - 1) if c >= 2 else s_av.wait(eng, n - 1, NCH - 1 + c)
            for x in range(2):
                s_am.wait(eng, n, 2 * c + x + 1)
                s_ah.done(eng.activation(att[:, c % 2, 0, C * x:C * x + C], att32[:, x, :], ACT.Copy))

        def state_hi(c):
            b = (c + 1) % 2
            s_S.wait(eng, n, c + 1)
            s_in.wait(eng, n, c) if c else s_in.wait(eng, n - 1)
            s_Sh.done(eng.activation(Shl[:, b, 0, :], S[:, :], ACT.Copy))

        def gate(half):
            s_pG.wait(eng, n, half + 1)
            s_gT.wait(eng, n - 1)
            s_tg.done(eng.activation(tg[:, half, :], big[:, half, :], ACT.Tanh, scale=half_rho_g[:, 0:1]))

        def square(t):
            s_y.wait(eng, n, t + 1)
            s_gs.wait(eng, n, t) if t else s_gs.wait(eng, n - 1)
            s_sq.done(eng.activation(ysq[:, :], y[:, t, :], ACT.Square))

        weights_hi(0)
        k_tokens(1)
        if tail:
            act_gated_hi(eng, n - 1)
        if ahead:
            act_mix_hi(eng, n + 1, 0)
        state_hi(0)
        gate(0)
        weights_hi(1)
        if ahead:
            act_mix_hi(eng, n + 1, 1)
        gate(1)
        state_hi(1)
        weights_hi(2)
        square(0)
        state_hi(2)
        weights_hi(3)
        state_hi(3)
        square(1)

    def pool_mix_lo(eng, n, m):
        s_mh.wait(eng, n, m + 1)
        s_ml.done(eng.tensor_tensor(mix[:, m, 1, :, :], mixf[:, m % 2, :, :], mix[:, m, 0, :, :], ALU.subtract))

    def pool_gated_lo(eng, n):
        for t in range(NT):
            s_ygh.wait(eng, n, t + 1)
            s_ygl.done(eng.tensor_tensor(yg[:, 1, :, rows(t)], ygT[:, :, rows(t)], yg[:, 0, :, rows(t)],
                                         ALU.subtract))

    def pool_block(eng, n, tail, ahead):
        def decay_state(c):
            s_S.wait(eng, n, c + 1)
            decay = ws
            if c == NCH - 2:
                s_wsf.wait(eng, n)
                decay = wsf
            s_Sw.done(eng.tensor_tensor(Sw[:, :].rearrange("p (g c) -> p g c", g=G),
                                        S[:, :].rearrange("p (g c) -> p g c", g=G),
                                        decay[:, :].unsqueeze(2).to_broadcast([P, G, P]), ALU.mult))

        def state_lo(c):
            s_Sh.wait(eng, n, c + 1)
            b = (c + 1) % 2
            s_Sl.done(eng.tensor_tensor(Shl[:, b, 1, :], S[:, :], Shl[:, b, 0, :], ALU.subtract))

        pool_mix_lo(eng, n, 2)
        pool_mix_lo(eng, n, 3)
        for t in range(NT):
            s_vwh.wait(eng, n, t + 1)
            s_vwl.done(eng.tensor_tensor(vw[:, t, 1, :], vw32[:, t, :], vw[:, t, 0, :], ALU.subtract))
        if tail:
            pool_gated_lo(eng, n - 1)
        for c in range(NCH):
            if ahead and c < 2:
                pool_mix_lo(eng, n + 1, c)
            state_lo(c)
            decay_state(c)

    def x_rows(x, n):
        return x[bass.ds(n * NT, NT), :, :].rearrange("t p c -> p t c")

    def sp_block(eng, n, tail, ahead, load):
        s_sc.wait_apart(eng, n - 1)
        s_kl.wait_apart(eng, n)
        for b in range(8):
            p = b % 2
            s_kx.done(eng.dma_start(kx[N * b:N * b + N, :, :, p, :],
                                    kT[N * b:N * b + N, :, :, :].rearrange("p a g (c j) -> p (a g) c j", j=Q)))
        s_rl.wait_apart(eng, n)
        for q in range(4):
            s_rx.done(eng.dma_start(rx[32 * q:32 * q + 32, :, :, q, :], rT[32 * q:32 * q + 32, :, :, :]))
        for t in range(NT):
            s_vl.wait_apart(eng, n, t + 1)
            s_av.wait_apart(eng, n - 1, 2 * t + 2)
            for c in range(2):
                for p in range(2):
                    s_vbd[t].done(eng.dma_start(vbd[Q * p:Q * p + Q, t, c, :, p, :], vN[Q * c:Q * c + Q, t, :, p, :]))
        if load:
            s_X.wait_apart(eng, n + 1)
            s_xa.done(eng.dma_start(xa[:, :, :], x_rows(x, n + 2)))
        if tail:
            s_x1.wait_apart(eng, n - 1)
            s_st.done(eng.dma_start(x_rows(x1_out, n - 1), x1[:, :, :]))
            s_st.wait_apart(eng, n - 1)
        s_xr.done(eng.dma_start(x1[:, :, :], x_rows(x, n)))

    def every_block(eng, block_fn, extra=False):
        if extra:
            block_fn(eng, 0, False, True, True)
            with eng.Fori(1, nb - 2) as n:
                block_fn(eng, n, True, True, True)
            block_fn(eng, nb - 2, True, True, False)
            block_fn(eng, nb - 1, True, False, False)
        else:
            block_fn(eng, 0, False, True)
            with eng.Fori(1, nb - 1) as n:
                block_fn(eng, n, True, True)
            block_fn(eng, nb - 1, True, False)

    with nc.Block() as block:
        @block.sync
        def _(eng):
            s_xa.done(eng.dma_start(xa[:, :, :], x_rows(x, 0)))
            s_X.wait(eng, 0)
            s_xa.done(eng.dma_start(xa[:, :, :], x_rows(x, 1)))
            s_zero.wait(eng, 4)
            every_block(eng, sp_block, True)
            s_x1.wait(eng, nb - 1)
            s_st.done(eng.dma_start(x_rows(x1_out, nb - 1), x1[:, :, :]))
            s_st.wait(eng, nb - 1)

        @block.tensor
        def _(eng):
            for t in range(NT):
                pe_X(eng, 0, t)
            s_zero.wait(eng, 1)
            every_block(eng, pe_block)
            s_x1.wait(eng, nb - 2)
            pe_tail_yT(eng, nb - 1)
            for t in range(NT):
                pe_tail_Wo(eng, nb - 1, t)

        @block.vector
        def _(eng):
            in_turn(dve_ln(eng, 0))
            s_carry.done(eng.memset(xnT[:, :, 0:1], 0.0))
            dve_dx(eng, 0)
            for m in range(2):
                in_turn(dve_mix(eng, 0, m))
            every_block(eng, dve_block)
            in_turn(dve_normalize(eng, nb - 1))
            dve_gated(eng, nb - 1)
            for t in range(NT):
                dve_residual(eng, nb - 1, t)

        @block.scalar
        def _(eng):
            act_norm(eng, 0)
            act_xT(eng, 0)
            for m in range(2):
                act_mix_hi(eng, 0, m)
            every_block(eng, act_block)
            s_ygl.wait(eng, nb - 2)
            act_gated(eng, nb - 1)
            act_gated_hi(eng, nb - 1)

        @block.gpsimd
        def _(eng):
            s_zero.done(eng.memset(Sw[:, :], 0.0))
            s_zero.done(eng.memset(Shl[:, 0, :, :].rearrange("p a c -> p (a c)").bitcast(F32), 0.0))
            s_zero.done(eng.memset(kx[:, :, :, :, :].rearrange("p a c b t -> p (a c b t)").bitcast(F32), 0.0))
            s_zero.done(eng.memset(rx[:, :, :, :, :].rearrange("p a g b t -> p (a g b t)").bitcast(F32), 0.0))
            s_zero.done(eng.memset(vbd[:, :, :, :, :, :].rearrange("p t c a b d -> p (t c a b d)").bitcast(F32), 0.0))
            for m in range(2):
                pool_mix_lo(eng, 0, m)
            every_block(eng, pool_block)
            pool_gated_lo(eng, nb - 1)


def ffn(nc, ctx, xio_in, out, W0, bias0, W1, bias1, consts, nb):

    def sb(name, shape, dt=F32):
        return ctx.enter_context(nc.sbuf_tensor(name, shape, dt))

    def ps(name, shape, dt=F32):
        return ctx.enter_context(nc.psum_tensor(name, shape, dt))

    s_passed = ctx.enter_context(nc.semaphore("f_passed"))

    def step(name, per, unit=1):
        return Step(nc, ctx, name, per, unit, s_passed)

    def rows(t):
        return slice(P * t, P * t + P)

    NH = HID // P
    ident16 = sb("f_ident16", [P, P], F16)
    W0T = sb("W0T", [P, 2, G, HID], F16)
    W1T = sb("W1T", [P, 2, NH, C], F16)
    rho = sb("f_rho", [P, 2])
    scl = sb("f_scl", [P, 2])
    b0 = sb("b0", [P, NH])
    b1 = sb("b1", [P, C])
    f_const = step("f_const", 1, 16)
    f_b1 = step("f_b1", 1, 16)
    f_scale = step("f_scale", 1)

    def load_first(eng):
        f_const.done(eng.dma_start(ident16[:, :], consts["ident16"]))
        f_const.done(eng.dma_start(b0[:, :], bias0.rearrange("(g p) -> p g", p=P), allow_slow_non_contiguous=True))

    def load_last(eng):
        f_b1.done(eng.dma_start(b1[:, :], bias1.partition_broadcast(P)))
        f_b1.wait(eng, 0)

    units = [(W0[C * u:C * u + C, :], 0, W0T[:, :, :, C * u:C * u + C]) for u in range(4)]
    units += [(W1[:, C * u:C * u + C], 1, W1T[:, :, G * u:G * u + G, :]) for u in range(4)]
    load_weights(nc, ctx, "f", units[0:4], rho[:, 0:1], scl[:, 0:1], None, ident16[:, :], None,
                 load_first, load_last, f_const)
    load_weights(nc, ctx, "h", [(a, 0, c) for a, _, c in units[4:8]], rho[:, 1:2], scl[:, 1:2], None,
                 ident16[:, :], None, lambda eng: None, lambda eng: None, f_const)

    x1 = sb("f_x1", [P, 2, FN, C])
    bn = sb("f_bn", [P, FN, 6])
    mv = sb("f_mv", [P, FN, 2])
    ln_a, ln_r, ln_t, ln_n = (sb(f"f_ln_{c}", [P, FN]) for c in "artn")
    xh = sb("f_xh", [P, FN, C], F16)
    xT = sb("f_xT", [P, G, FT], F16)
    hT = sb("f_hT", [P, NH, FT], F16)
    e16 = sb("f_e16", [P, FN, C], F16)
    o = sb("f_o", [P, FN, C])
    xr = sb("f_xr", [P, FN, C])

    up = ps("up_ps", [P, 4, C])
    down = ps("down_ps", [P, 2, C])
    trp = ps("f_trp", [P, 2, 2 * C], F16)

    s_ld = step("f_ld", 1, 16)
    s_rs = step("f_rs", 1, 16)
    s_st = step("f_st", 1, 16)
    s_bn = step("f_sbn", 2 * FN)
    s_ln = step("f_sln", 2 + RSQRT_STEPS)
    s_xh = step("f_sxh", FN)
    s_tr = step("f_str", 2)
    s_xT = step("f_sxT", 2)
    s_up = step("f_sup", NH)
    s_h = step("f_sh", NH)
    s_dn = step("f_sdn", FN)
    s_e = step("f_se", FN)
    s_o = step("f_so", FN)

    def blk(x, n):
        return x[bass.ds(n * FN, FN), :, :].rearrange("t p c -> p t c")

    def sp_block(eng, n, load):
        s_o.wait_apart(eng, n - 1)
        s_rs.done(eng.dma_start(xr[:, :, :], blk(xio_in, n)))
        if load:
            s_xh.wait_apart(eng, n + 1)
            s_ld.done(eng.dma_start(x1[:, 0, :, :], blk(xio_in, n + 2)))
        s_o.wait_apart(eng, n)
        s_st.done(eng.dma_start(blk(out, n), o[:, :, :]))

    def dve_ln(eng, n):
        s_ld.wait(eng, n)
        for t in range(FN):
            s_bn.done(eng.bn_stats(bn[:, t, :], x1[:, 0, t, :]))
        for t in range(FN):
            s_bn.wait_apart(eng, n, t + 1)
            s_bn.done(eng.bn_aggr(mv[:, t, :], bn[:, t, :]))
        s_bn.wait(eng, n)
        s_ln.done(eng.tensor_scalar(ln_a[:, :], mv[:, :, 1], LN_EPS, None, ALU.add))
        s_ln.wait(eng, n, 1)
        yield from rsqrt(eng, s_ln, n, ln_a[:, :], ln_r[:, :], ln_t[:, :], 1)
        s_ln.done(eng.scalar_tensor_tensor(out=ln_n[:, :], in0=mv[:, :, 0], scalar=-1.0, in1=ln_r[:, :],
                                           op0=ALU.mult, op1=ALU.mult))

    def dve_xT(eng, n):
        s_up.wait(eng, n - 1)
        for k in range(2):
            s_tr.wait(eng, n, k + 1)
            s_xT.done(eng.tensor_copy(xT[:, 2 * k:2 * k + 2, :], trp[:, k, :].rearrange("p (g t) -> p g t", g=2)))

    def dve_block(eng, n, ahead):
        if ahead:
            in_turn(dve_ln(eng, n + 1))
            dve_xT(eng, n + 1)
        for t in range(FN):
            s_dn.wait(eng, n, t + 1)
            s_o.wait(eng, n - 1, t + 1)
            s_e.done(eng.scalar_tensor_tensor(out=e16[:, t, :], in0=down[:, t % 2, :], scalar=rho[:, 1:2],
                                              in1=b1[:, :], op0=ALU.mult, op1=ALU.add))

    def act_norm(eng, n):
        s_ln.wait(eng, n)
        s_tr.wait(eng, n - 1)
        for t in range(FN):
            s_xh.done(eng.activation(xh[:, t, :], x1[:, 0, t, :], ACT.Identity, bias=ln_n[:, t:t + 1],
                                     scale=ln_r[:, t:t + 1]))

    def act_block(eng, n, ahead):
        s_dn.wait(eng, n - 1)
        for k in range(NH):
            if k == NH // 2 and ahead:
                act_norm(eng, n + 1)
            s_up.wait(eng, n, k + 1)
            s_h.done(eng.activation(hT[:, k, :], up[:, k % 4, :], ACT.Gelu, bias=b0[:, k:k + 1], scale=rho[:, 0:1]))

    def pe_transposes(eng, n):
        s_xh.wait(eng, n)
        for k in range(2):
            s_xT.wait(eng, n - 1, k + 1)
            for gg in range(2):
                for t in range(FN):
                    tr = eng.transpose(trp[:, k, gg * FT + P * t:gg * FT + P * t + P], xh[:, t, rows(2 * k + gg)],
                                       ident16[:, :])
            s_tr.done(tr)

    def pe_block(eng, n, ahead):
        s_xT.wait(eng, n)
        for k in range(NH):
            s_h.wait(eng, n, k - 3) if k >= 4 else s_h.wait(eng, n - 1, NH - 3 + k)
            for kk in range(G):
                for a in range(2):
                    mm = eng.matmul(up[:, k % 4, :], W0T[:, a, kk, rows(k)], xT[:, kk, :],
                                    start=(kk == 0 and a == 0), stop=(kk == G - 1 and a == 1))
            s_up.done(mm)
        if ahead:
            pe_transposes(eng, n + 1)
        for t in range(FN):
            s_e.wait(eng, n, t - 1) if t >= 2 else s_e.wait(eng, n - 1, FN - 1 + t)
            s_h.wait(eng, n)
            for k in range(NH):
                for a in range(2):
                    mm = eng.matmul(down[:, t % 2, :], hT[:, k, rows(t)], W1T[:, a, k, :],
                                    start=(k == 0 and a == 0), stop=(k == NH - 1 and a == 1))
            s_dn.done(mm)

    def pool_block(eng, n, ahead):
        s_rs.wait(eng, n)
        s_st.wait(eng, n - 1)
        for t in range(FN):
            s_e.wait(eng, n, t + 1)
            s_o.done(eng.tensor_tensor(o[:, t, :], e16[:, t, :], xr[:, t, :], ALU.add))

    def every_block(eng, fn):
        fn(eng, 0, True)
        with eng.Fori(1, nb - 1) as n:
            fn(eng, n, True)
        fn(eng, nb - 1, False)

    with nc.Block() as block:
        @block.sync
        def _(eng):
            s_ld.done(eng.dma_start(x1[:, 0, :, :], blk(xio_in, 0)))
            s_xh.wait(eng, 0)
            s_ld.done(eng.dma_start(x1[:, 0, :, :], blk(xio_in, 1)))
            sp_block(eng, 0, True)
            with eng.Fori(1, nb - 2) as n:
                sp_block(eng, n, True)
            sp_block(eng, nb - 2, False)
            sp_block(eng, nb - 1, False)
            s_st.wait(eng, nb - 1)

        @block.vector
        def _(eng):
            f_scale.done(eng.tensor_scalar(rho[:, :], rho[:, :], 1.0 / KS, None, ALU.mult))
            f_scale.wait(eng, 0)
            in_turn(dve_ln(eng, 0))
            dve_xT(eng, 0)
            every_block(eng, dve_block)

        @block.scalar
        def _(eng):
            f_scale.wait(eng, 0)
            act_norm(eng, 0)
            every_block(eng, act_block)

        @block.tensor
        def _(eng):
            pe_transposes(eng, 0)
            every_block(eng, pe_block)

        @block.gpsimd
        def _(eng):
            every_block(eng, pool_block)


def build(nc, a, consts, x1, out):
    tiles = lambda v: v.rearrange("b (t p) c -> (b t) p c", p=P)
    ntok = a["L0_attn_x"].shape[0] * a["L0_attn_x"].shape[1]
    with ExitStack() as ctx:
        attention(nc, ctx, tiles(a["L0_attn_x"]), x1,
                  [a[f"L0_attn_time_maa_{m}"] for m in "krvg"], [a[f"L0_attn_W{m}"] for m in "krvgo"],
                  a["L0_attn_time_decay"], a["L0_attn_time_faaaa"], a["L0_attn_gamma"], a["L0_attn_beta"],
                  consts, ntok // BT)
    with ExitStack() as ctx:
        ffn(nc, ctx, x1, tiles(out), a["L0_ffn_W0"], a["L0_ffn_bias0"], a["L0_ffn_W1"], a["L0_ffn_bias1"],
            consts, ntok // FT)


_INS = ['L0_attn_x', 'L0_attn_time_maa_k', 'L0_attn_time_maa_v', 'L0_attn_time_maa_r', 'L0_attn_time_maa_g',
        'L0_attn_time_decay', 'L0_attn_time_faaaa', 'L0_attn_Wr', 'L0_attn_Wk', 'L0_attn_Wv', 'L0_attn_Wg',
        'L0_attn_Wo', 'L0_attn_gamma', 'L0_attn_beta', 'L0_ffn_W0', 'L0_ffn_bias0', 'L0_ffn_W1', 'L0_ffn_bias1']


def constants():
    r = np.arange(P)
    i, j = np.arange(Q)[None, :], (r % Q)[:, None]
    same_head = (r[:, None] // N == r[None, :] // N).astype(np.float32)
    return {
        "ident": np.eye(P, dtype=np.float32),
        "ident16": np.eye(P, dtype=np.float16),
        "centring": (np.eye(P) - same_head / N).astype(np.float32),
        "headmask": same_head,
        "dist": np.maximum(i - j - 1, 0).astype(np.float32),
        "after": ((i > j) * ATT_S).astype(np.float32),
        "same": ((i == j) * ATT_S).astype(np.float32),
        "ages": np.stack([-(r % Q), -(Q - 1 - r % Q)], 1).astype(np.float32),
    }


def kernel(**inputs):
    import concourse.bacc as bacc
    from concourse.bass_utils import run_bass_kernel_spmd

    nc = bacc.Bacc("TRN2", target_bir_lowering=False, num_devices=1)
    arrays, aps, consts = {}, {}, {}
    for name in _INS:
        v = np.ascontiguousarray(inputs[name])
        arrays[f"in_{name}"] = v
        aps[name] = nc.dram_tensor(f"in_{name}", v.shape, mybir.dt.from_np(v.dtype), kind="ExternalInput").ap()
    for name, v in constants().items():
        v = np.ascontiguousarray(v)
        arrays[f"const_{name}"] = v
        consts[name] = nc.dram_tensor(f"const_{name}", v.shape, mybir.dt.from_np(v.dtype), kind="ExternalInput").ap()
    shape = inputs["L0_attn_x"].shape
    tiles = shape[0] * shape[1] // P
    x1 = nc.dram_tensor("x1_dram", (tiles, P, C), F32, kind="Internal").ap()
    out = nc.dram_tensor("out", shape, F32, kind="ExternalOutput").ap()
    build(nc, aps, consts, x1, out)
    r = run_bass_kernel_spmd(nc, [arrays], core_ids=[0])
    return r.results[0]["out"]
```

```python
from contextlib import ExitStack

import numpy as np

import concourse.bass as bass
from concourse import mybir

F32, F16, I32 = mybir.dt.float32, mybir.dt.float16, mybir.dt.int32
ALU = mybir.AluOpType
ACT = mybir.ActivationFunctionType
AX = mybir.AxisListType

P = 128
C = 512
H, N = 32, 16
G = C // P
HID = 2048
Q = 64
BT, NT = 256, 2
NCH = BT // Q
T = 2048
FT, FN = 512, 4
LN_EPS = 1e-5
GN_EPS = 1e-5 * 144
KS = 2.0 ** 10
ATT_S = 2.0 ** -5
STATE_S = 2.0 ** -7
YG_S = 2.0 ** -1
EXP_BITS = 0x7F800000
RSQRT_MAGIC = 0x5F3759DF


class Step:

    def __init__(self, nc, ctx, name, per, unit=1, passed=None):
        self.sem = ctx.enter_context(nc.semaphore(name))
        self.per, self.unit = per, unit
        self.passed = passed

    def done(self, instruction):
        return instruction.then_inc(self.sem, self.unit)

    def wait(self, eng, block, k=None):
        value = (block * self.per + (self.per if k is None else k)) * self.unit
        if not isinstance(value, int) or value > 0:
            eng.wait_ge(self.sem, value)

    def wait_apart(self, eng, block, k=None):
        self.wait(eng, block, k)
        if not isinstance(block, int):
            eng.sem_inc(self.passed, 1)


def rsqrt(eng, step, block, x, y, t, first):
    half = dict(scalar=-0.5, in1=x, op0=ALU.mult, op1=ALU.mult)
    newton = [lambda: eng.tensor_tensor(t, y, y, ALU.mult),
              lambda: eng.scalar_tensor_tensor(out=t, in0=t, **half),
              lambda: eng.scalar_tensor_tensor(out=y, in0=t, scalar=1.5, in1=y, op0=ALU.add, op1=ALU.mult)]
    guess = [lambda: eng.tensor_scalar(t.bitcast(I32), x.bitcast(I32), 1, None, ALU.logical_shift_right),
             lambda: eng.tensor_scalar(y.bitcast(I32), t.bitcast(I32), -1.0, float(RSQRT_MAGIC), ALU.mult, ALU.add)]
    for k, instruction in enumerate(guess + 3 * newton):
        step.done(instruction())
        yield
        step.wait(eng, block, first + k + 1)


def in_turn(*parts):
    parts = list(parts)
    while parts:
        parts = [part for part in parts if next(part, parts) is None]


RSQRT_STEPS = 11


class WeightUnits:

    def __init__(self, nc, ctx, tag, sources, slots, rounds, shares, centre=None):
        nu = len(sources)
        self.sources, self.rounds, self.centre, self.nr = sources, rounds, centre, len(slots)
        self.raw = [slots[u % len(slots)] for u in range(nu)]
        self.junk = ctx.enter_context(nc.sbuf_tensor(f"{tag}junk", [P, C], F32))
        self.bn = ctx.enter_context(nc.sbuf_tensor(f"{tag}bn", [P, nu, G, 6], F32))
        self.mv = ctx.enter_context(nc.sbuf_tensor(f"{tag}mv", [P, nu, G, 2], F32))
        self.sums = ctx.enter_context(nc.sbuf_tensor(f"{tag}sums", [P, nu, G], F32))
        self.landed = [Step(nc, ctx, f"{tag}landed{u}", 1, 16) for u in range(nu)]
        self.s_cent = Step(nc, ctx, f"{tag}cent", 1)
        self.s_sum = Step(nc, ctx, f"{tag}sum", 1)
        self.s_bn = Step(nc, ctx, f"{tag}bns", 1)
        self.nbn = 0
        self.dve_units = [[u for u in r if u != centre][-share:] for r, share in zip(rounds, shares)]
        self.act_units = [[u for u in r if u not in d and u != centre] + [u for u in r if u == centre]
                          for r, d in zip(rounds, self.dve_units)]
        self.act_order = [u for a in self.act_units for u in a]

    def load(self, eng, u):
        self.landed[u].done(eng.dma_start(self.raw[u], self.sources[u].rearrange("(b p) c -> p b c", p=P)))

    def act_squares(self, eng, k):
        for u in self.act_units[k]:
            self.landed[u].wait(eng, 0)
            if u == self.centre:
                self.s_cent.wait(eng, 0)
            for b in range(G):
                self.s_sum.wait(eng, self.act_order.index(u) * G + b - 1)
                self.s_sum.done(eng.activation(self.junk[:, :], self.raw[u][:, b, :], ACT.Square,
                                               accum_out=self.sums[:, u, b:b + 1]))

    def dve_squares(self, eng, k):
        bn, mv, sums, units = self.bn, self.mv, self.sums, self.dve_units[k]

        def each(instruction, per_group=False):
            for u in units:
                for b in range(G if per_group else 1):
                    self.s_bn.done(instruction(u, b) if per_group else instruction(u))
                    self.nbn += 1
            self.s_bn.wait(eng, self.nbn - 1)

        for u in units:
            self.landed[u].wait(eng, 0)
        each(lambda u, b: eng.bn_stats(bn[:, u, b, :], self.raw[u][:, b, :]), True)
        each(lambda u, b: eng.bn_aggr(mv[:, u, b, :], bn[:, u, b, :]), True)
        each(lambda u: eng.tensor_tensor(sums[:, u, :], mv[:, u, :, 0], mv[:, u, :, 0], ALU.mult))
        each(lambda u: eng.tensor_tensor(sums[:, u, :], sums[:, u, :], mv[:, u, :, 1], ALU.add))
        each(lambda u: eng.tensor_scalar(sums[:, u, :], sums[:, u, :], float(C), None, ALU.mult))

    def wait_act_sum(self, eng, u):
        if u in self.act_order:
            self.s_sum.wait(eng, self.act_order.index(u) * G + G - 1)


def load_weights(nc, tag, wu, cols, places, rho, scl, ident16, centring, load_first, load_last, s_const,
                 begun=0, aside=None):
    nu, nr, rounds, raw, landed, centre = len(cols), wu.nr, wu.rounds, wu.raw, wu.landed, wu.centre
    with ExitStack() as own:
        nat = own.enter_context(nc.sbuf_tensor(f"{tag}nat", [P, 2, 2, G, C], F16))
        most = own.enter_context(nc.sbuf_tensor(f"{tag}most", [P, rho.shape[1]], F32))
        tps = own.enter_context(nc.psum_tensor(f"{tag}tps", [P, 4, 2 * C], F16))
        cps = tps[:, :, :].bitcast(F32)
        s_cen = Step(nc, own, f"{tag}cen", 1)
        s_max = Step(nc, own, f"{tag}max", 1)
        s_all = Step(nc, own, f"{tag}all", 1)
        s_norm = Step(nc, own, f"{tag}norm", 1)
        s_scl = Step(nc, own, f"{tag}scl", 4)
        s_hi = Step(nc, own, f"{tag}hi", 1)
        s_lo = Step(nc, own, f"{tag}lo", 1)
        s_tr = Step(nc, own, f"{tag}tr", 4)
        s_evd = Step(nc, own, f"{tag}evd", 2)
        s_eva = Step(nc, own, f"{tag}eva", 2)

        def other(k, engine, eng):
            if aside and aside[0] == k and engine in aside[1]:
                aside[1][engine](eng)

        def cspan(k):
            cs = [cols[u] for u in rounds[k]]
            return slice(min(cs), max(cs) + 1)

        def evacuate(eng, u, hl, step):
            dst = places[u]
            for half in range(2):
                s_tr.wait(eng, u, 2 * hl + half + 1)
                out, src = dst[:, hl, 2 * half:2 * half + 2, :], tps[:, 2 * hl + half, :].rearrange(
                    "p (k c) -> p k c", k=2)
                step.done(eng.activation(out, src, ACT.Copy) if hl else eng.tensor_copy(out, src))

        with nc.Block() as block:

            @block.sync
            def _(eng):
                load_first(eng)
                for u in sorted(range(begun, nu), key=lambda u: u != centre):
                    if u >= nr:
                        s_lo.wait(eng, u - nr)
                    wu.load(eng, u)
                load_last(eng)

            @block.scalar
            def _(eng):
                other(0, "scalar", eng)
                if not begun:
                    wu.act_squares(eng, 0)
                for k, units_k in enumerate(rounds):
                    s_all.wait(eng, k)
                    s_norm.done(eng.activation(rho[:, cspan(k)], most[:, cspan(k)], ACT.Sqrt))
                    for u in units_k:
                        s_scl.wait(eng, k)
                        s_tr.wait(eng, u - 2)
                        s_hi.done(eng.activation(nat[:, u % 2, 0, :, :], raw[u], ACT.Identity,
                                                 scale=scl[:, cols[u]:cols[u] + 1]))
                        if u != units_k[0]:
                            evacuate(eng, u - 1, 1, s_eva)
                    evacuate(eng, units_k[-1], 1, s_eva)
                    if k + 1 < len(rounds):
                        other(k + 1, "scalar", eng)
                        wu.act_squares(eng, k + 1)

            @block.gpsimd
            def _(eng):
                other(0, "gpsimd", eng)
                for k in range(len(rounds)):
                    s_max.wait(eng, cspan(k).stop - 1)
                    s_all.done(eng.partition_all_reduce(most[:, cspan(k)], most[:, cspan(k)], P,
                                                        bass.bass_isa.ReduceOp.max))

            @block.vector
            def _(eng):
                other(0, "vector", eng)
                if centre is not None:
                    s_cen.wait(eng, 0)
                    wu.s_cent.done(eng.tensor_copy(raw[centre], cps))
                if not begun:
                    wu.dve_squares(eng, 0)
                for k, units_k in enumerate(rounds):
                    for w in range(cspan(k).start, cspan(k).stop):
                        us = [u for u in units_k if cols[u] == w]
                        for u in us:
                            wu.wait_act_sum(eng, u)
                        s_max.done(eng.tensor_reduce(most[:, w:w + 1], wu.sums[:, us[0]:us[-1] + 1, :], AX.XY, ALU.max))
                    s_norm.wait(eng, k)
                    rk, sk = rho[:, cspan(k)], scl[:, cspan(k)]
                    s_scl.done(eng.tensor_scalar(rk, rk, 1e-12, None, ALU.max))
                    s_scl.wait(eng, k, 1)
                    s_scl.done(eng.tensor_scalar(rk.bitcast(I32), rk.bitcast(I32), EXP_BITS, None, ALU.bitwise_and))
                    s_scl.wait(eng, k, 2)
                    s_scl.done(eng.reciprocal(sk, rk))
                    s_scl.wait(eng, k, 3)
                    s_scl.done(eng.tensor_scalar(sk, sk, KS, None, ALU.mult))
                    s_scl.wait(eng, k)
                    for u in units_k:
                        if u != units_k[0]:
                            evacuate(eng, u - 1, 0, s_evd)
                        s_hi.wait(eng, u)
                        s_lo.done(eng.scalar_tensor_tensor(
                            out=nat[:, u % 2, 1, :, :].rearrange("p b c -> p (b c)"),
                            in0=raw[u].rearrange("p b c -> p (b c)"),
                            scalar=scl[:, cols[u]:cols[u] + 1],
                            in1=nat[:, u % 2, 0, :, :].rearrange("p b c -> p (b c)"),
                            op0=ALU.mult, op1=ALU.subtract))
                    evacuate(eng, units_k[-1], 0, s_evd)
                    if k + 1 < len(rounds):
                        other(k + 1, "vector", eng)
                        wu.dve_squares(eng, k + 1)

            @block.tensor
            def _(eng):
                other(0, "tensor", eng)
                s_const.wait(eng, 1)
                if centre is not None:
                    landed[centre].wait(eng, 0)
                    for b in range(G):
                        mm = eng.matmul(cps[:, b, :], centring, raw[centre][:, b, :], start=True, stop=True)
                    s_cen.done(mm)
                for u in range(nu):
                    for k, units_k in enumerate(rounds):
                        if k and u == units_k[0]:
                            other(k, "tensor", eng)
                    for hl in range(2):
                        (s_lo if hl else s_hi).wait(eng, u)
                        for half in range(2):
                            (s_eva if hl else s_evd).wait(eng, u - 1, half + 1)
                            for kk in range(2):
                                for b in range(G):
                                    k = 2 * half + kk
                                    tr = eng.transpose(tps[:, 2 * hl + half, kk * C + b * P:kk * C + (b + 1) * P],
                                                       nat[:, u % 2, hl, b, k * P:(k + 1) * P], ident16)
                            s_tr.done(tr)


def attention(nc, ctx, x, x1_out, maas, weights, decay, bonus, gamma, beta, consts, nb, store, next_units):

    def sb(name, shape, dt=F32):
        return ctx.enter_context(nc.sbuf_tensor(name, shape, dt))

    def ps(name, shape, dt=F32):
        return ctx.enter_context(nc.psum_tensor(name, shape, dt))

    s_passed = ctx.enter_context(nc.semaphore("a_passed"))

    def step(name, per, unit=1):
        return Step(nc, ctx, name, per, unit, s_passed)

    ident = sb("ident", [P, P])
    ident16 = sb("ident16", [P, P], F16)
    centring = sb("centring", [P, P])
    WT = sb("WT", [P, 5, 2, G, C], F16)
    rho = sb("rho", [P, 5])
    scl = sb("scl", [P, 5])
    maa = sb("maa", [P, 4, G])
    wmask = sb("wmask", [P, NT * 8, Q])
    headmask = sb("headmask", [P, P])
    wb = sb("wb", [P, H])
    wk = sb("wk", [P, H])
    ws = sb("ws", [P, G])
    wsf = sb("wsf", [P, G])
    flag = sb("flag", [P, nb + 1])
    gam = sb("gam", [P, G])
    bet = sb("bet", [P, G])
    gn_eps = sb("gn_eps", [P, 1])
    half_rho_g = sb("half_rho_g", [P, 1])
    out_scale = sb("out_scale", [P, 1])
    s_const = step("s_const", 1, 16)
    s_ident = step("s_ident", 1, 16)
    s_maa = step("s_maa", 4, 16)

    xa = sb("xa", [P, NT, C])
    s_xa = step("s_xa", 1, 16)

    def x_rows(x, n):
        return x[bass.ds(n * NT, NT), :, :].rearrange("t p c -> p t c")

    K_, R_, V_, G_, O_ = range(5)

    dist = sb("dist", [P, Q])
    after = sb("after", [P, Q])
    same = sb("same", [P, Q])
    ages = sb("ages", [P, 2])
    ep = sb("ep", [P, NT * 8])
    up = sb("up", [P, NT * 8])
    un = sb("un", [P, H])
    en = sb("en", [P, H])
    ec = sb("ec", [P, G])
    diag = sb("diag", [P, NT * 8, Q])
    s_tin = step("t_in", 1, 16)
    s_e = step("t_e", 1)
    s_n = step("t_n", 1)
    s_x = step("t_x", 1)
    s_t = step("t_t", 1)
    loads = [(dist[:, :], consts["dist"]), (after[:, :], consts["after"]), (same[:, :], consts["same"]),
             (ages[:, :], consts["ages"]), (headmask[:, :], consts["headmask"]),
             (en[:, :], decay.rearrange("h o -> (h o)").partition_broadcast(P)),
             (un[:, :], bonus.rearrange("h o -> (h o)").partition_broadcast(P)),
             (gam[:, :], gamma.rearrange("(g p) -> p g", p=P)), (bet[:, :], beta.rearrange("(g p) -> p g", p=P))]
    for h in range(8):
        loads.append((ec[N * h:N * h + N, :],
                      decay.rearrange("(g h) o -> h (g o)", h=8)[h].partition_broadcast(N)))

    def load_first(eng):
        s_xa.done(eng.dma_start(xa[:, :, :], x_rows(x, 0)))
        s_ident.done(eng.dma_start(ident[:, :], consts["ident"]))
        s_const.done(eng.dma_start(centring[:, :], consts["centring"]))
        s_const.done(eng.dma_start(ident16[:, :], consts["ident16"]))
        for m, v in enumerate(maas):
            s_maa.done(eng.dma_start(maa[:, m, :], v.rearrange("a b (g p) -> p (a b g)", p=P),
                                     allow_slow_non_contiguous=True))

    def load_last(eng):
        for dst, src in loads:
            s_tin.done(eng.dma_start(dst, src, allow_slow_non_contiguous=True))
        s_tin.wait(eng, len(loads) - 1)

    def act_tables(eng):
        for t in (en, ec):
            s_e.done(eng.activation(t[:, :], t[:, :], ACT.Exp))
        s_n.wait(eng, 5)
        for q in range(NT * 8):
            s_x.done(eng.activation(wmask[:, q, :], dist[:, :], ACT.Exp, scale=ep[:, q:q + 1]))
        s_x.done(eng.activation(wb[:, :], wb[:, :], ACT.Exp))
        s_x.done(eng.activation(wk[:, :], wk[:, :], ACT.Exp))
        s_x.done(eng.activation(ws[:, :], ec[:, :], ACT.Exp, scale=-float(Q)))

    def dve_tables(eng):
        nq = NT * 8
        s_e.wait(eng, 1)
        s_n.done(eng.tensor_scalar(wb[:, :], en[:, :], ages[:, 0:1], None, ALU.mult))
        s_n.done(eng.tensor_scalar(wk[:, :], en[:, :], ages[:, 1:2], None, ALU.mult))
        for p in range(2):
            half = slice(Q * p, Q * p + Q)
            s_n.done(eng.tensor_scalar(ep[half, :], en[half, p:H:2], -1.0, None, ALU.mult))
            s_n.done(eng.tensor_copy(up[half, :], un[half, p:H:2]))
        s_n.wait(eng, 5)
        s_n.done(eng.tensor_tensor(diag[:, :, :], same[:, :].unsqueeze(1).to_broadcast([P, nq, Q]),
                                   up[:, :].unsqueeze(2).to_broadcast([P, nq, Q]), ALU.mult))
        s_x.wait(eng, nq + 2)
        s_t.done(eng.tensor_tensor(wmask[:, :, :], wmask[:, :, :],
                                   after[:, :].unsqueeze(1).to_broadcast([P, nq, Q]), ALU.mult))
        s_t.wait(eng, 0)
        s_n.wait(eng, 6)
        s_t.done(eng.tensor_tensor(wmask[:, :, :], wmask[:, :, :], diag[:, :, :], ALU.add))
        s_t.done(eng.tensor_scalar(wb[:, :], wb[:, :], ATT_S / STATE_S, None, ALU.mult))
        s_t.done(eng.tensor_scalar(wk[:, :], wk[:, :], STATE_S / KS, None, ALU.mult))
        s_t.done(eng.tensor_scalar(gam[:, :], gam[:, :], YG_S / (2 * KS), None, ALU.mult))
        s_t.done(eng.tensor_scalar(bet[:, :], bet[:, :], YG_S / (2 * KS), None, ALU.mult))
        s_t.done(eng.memset(flag[:, :], 1.0))
        s_t.wait(eng, 6)
        s_t.done(eng.memset(flag[:, 0:nb + 1:T // BT], 0.0))
        s_t.done(eng.tensor_tensor(gn_eps[:, :], rho[:, K_:K_ + 1], rho[:, R_:R_ + 1], ALU.mult))
        s_t.wait(eng, 8)
        s_t.done(eng.tensor_tensor(gn_eps[:, :], gn_eps[:, :], rho[:, V_:V_ + 1], ALU.mult))
        s_t.wait(eng, 9)
        s_t.done(eng.reciprocal(gn_eps[:, :], gn_eps[:, :]))
        s_t.wait(eng, 10)
        s_t.done(eng.tensor_tensor(gn_eps[:, :], gn_eps[:, :], gn_eps[:, :], ALU.mult))
        s_t.wait(eng, 11)
        s_t.done(eng.tensor_scalar(gn_eps[:, :], gn_eps[:, :], GN_EPS * ATT_S ** 2, None, ALU.mult))
        s_t.done(eng.tensor_scalar(half_rho_g[:, :], rho[:, G_:G_ + 1], 0.5 / KS, None, ALU.mult))
        s_t.done(eng.tensor_tensor(out_scale[:, :], rho[:, G_:G_ + 1], rho[:, O_:O_ + 1], ALU.mult))
        s_t.wait(eng, 14)
        s_t.done(eng.tensor_scalar(out_scale[:, :], out_scale[:, :], 1.0 / (KS * YG_S), None, ALU.mult))
        s_t.wait(eng, 15)

    bn = sb("bn", [P, NT, 6])
    mv = sb("mv", [P, NT, 2])
    ln_a, ln_r, ln_t, ln_n = (sb(f"ln_{c}", [P, NT]) for c in "artn")
    xnT = sb("xnT", [P, G, BT + 1])
    dx = sb("dx", [P, G, BT])
    mixf = sb("mixf", [P, 2, G, BT])
    mix = sb("mix", [P, 4, 2, G, BT], F16)
    big = ps("big", [P, 2, C])

    s_xr = step("s_xr", 1, 16)
    s_st = step("s_st", 1, 16)
    s_kx = step("s_kx", 8, 16)
    s_rx = step("s_rx", 4, 16)
    s_vbd = [step(f"s_vbd{t}", 4, 16) for t in range(NT)]
    s_bn = step("s_bn", 4)
    s_ln = step("s_ln", 2 + RSQRT_STEPS)
    s_xn = step("s_xn", NT)
    s_X = step("s_X", NT)
    s_xT = step("s_xT", NT)
    s_carry = step("s_carry", 1)
    s_dx = step("s_dx", 1)
    s_mix = step("s_mix", 4)
    s_mh = step("s_mh", 4)
    s_ml = step("s_ml", 4)
    s_pK = step("s_pK", 2)
    s_pR = step("s_pR", 2)
    s_pG = step("s_pG", 2)
    s_pV = step("s_pV", NT)
    s_kh = step("s_kh", 2)
    s_kl = step("s_kl", 2)
    s_rh = step("s_rh", 2)
    s_rl = step("s_rl", 2)
    s_vh = step("s_vh", NT)
    s_vl = step("s_vl", NT)
    s_vw = step("s_vw", NT)
    s_vwh = step("s_vwh", NT)
    s_vwl = step("s_vwl", NT)
    s_kt = step("s_kt", NT)
    s_kN = step("s_kN", NT)
    s_tg = step("s_tg", 2)
    s_gT = step("s_gT", 2)
    s_sc = step("s_sc", 2 * NCH)
    s_am = step("s_am", 2 * NCH)
    s_ah = step("s_ah", 2 * NCH)
    s_al = step("s_al", 2 * NCH)
    s_av = step("s_av", NCH)
    s_in = step("s_in", NCH)
    s_kv = step("s_kv", NCH)
    s_km = step("s_km", NCH)
    s_S = step("s_S", NCH)
    s_wsf = step("s_wsf", 1)
    s_Sh = step("s_Sh", NCH)
    s_Sl = step("s_Sl", NCH)
    s_Sw = step("s_Sw", NCH)
    s_yi = step("s_yi", NT)
    s_y = step("s_y", NT)
    s_sq = step("s_sq", NT)
    s_gs = step("s_gs", NT)
    s_gn = step("s_gn", 1 + RSQRT_STEPS)
    s_yn = step("s_yn", NT)
    s_yT = step("s_yT", NT)
    s_af = step("s_af", G)
    s_yg = step("s_yg", NT)
    s_ygh = step("s_ygh", NT)
    s_ygl = step("s_ygl", NT)
    s_Wo = step("s_Wo", NT)
    s_x1 = step("s_x1", NT)
    s_zero = step("s_zero", 1)

    PASSES = ((0, 0), (0, 1), (1, 0))
    def rows(t):
        return slice(P * t, P * t + P)


    def pe_project_T(eng, out, w, m, half):
        for gg in range(2):
            g = 2 * half + gg
            for i, (a, b) in enumerate(PASSES):
                for kk in range(G):
                    mm = eng.matmul(out[:, gg * BT:(gg + 1) * BT], WT[:, w, a, kk, rows(g)],
                                    mix[:, m, b, kk, :], start=(i == 0 and kk == 0), stop=(i == 2 and kk == G - 1))
        return mm

    def pe_X(eng, n, t):
        s_xn.wait(eng, n, t + 1)
        for g in range(G):
            tr = eng.transpose(big[:, t, rows(g)], xa[:, t, rows(g)], ident[:, :])
        s_X.done(tr)

    def pe_tail_yT(eng, n):
        for t in range(NT):
            s_yn.wait(eng, n, t + 1)
            for g in range(G):
                tr = eng.transpose(big[:, t, rows(g)], y[:, t, rows(g)], ident[:, :])
            s_yT.done(tr)

    def pe_tail_Wo(eng, n, t):
        s_ygl.wait(eng, n, t + 1)
        for i, (a, b) in enumerate(PASSES):
            for kk in range(G):
                mm = eng.matmul(big[:, t, :], yg[:, a, kk, rows(t)], WT[:, 4, b, kk, :],
                                start=(i == 0 and kk == 0), stop=(i == 2 and kk == G - 1))
        s_Wo.done(mm)

    def pe_block(eng, n, tail, ahead):
        def mixed(m):
            s_ml.wait(eng, n, m + 1)
            s_mh.wait(eng, n, m + 1)

        mixed(0)
        for half in range(2):
            s_am.wait(eng, n - 1, 2 * NCH - 1 + half)
            s_pK.done(pe_project_T(eng, sc[:, half, :], 0, 0, half))
        mixed(1)
        s_km.wait(eng, n - 1)
        for half in range(2):
            s_pR.done(pe_project_T(eng, big[:, half, :], 1, 1, half))

        def k_tokens(t):
            s_kN.wait(eng, n - 1) if t == 0 else s_kN.wait(eng, n, 1)
            s_kl.wait(eng, n)
            for hl in range(2):
                for g in range(G):
                    tr = eng.transpose(trp[:, hl * C + g * P:hl * C + (g + 1) * P], kT[:, hl, g, rows(t)],
                                       ident16[:, :])
            s_kt.done(tr)

        mixed(2)
        for t in range(NT):
            if t:
                k_tokens(0)
            (s_yi if t else s_y).wait(eng, n - 1)
            for i, (a, b) in enumerate(PASSES):
                for kk in range(G):
                    mm = eng.matmul(Y[:, t, :], mix[:, 2, a, kk, rows(t)], WT[:, 2, b, kk, :],
                                    start=(i == 0 and kk == 0), stop=(i == 2 and kk == G - 1))
            s_pV.done(mm)
            if t == 0:
                s_rl.wait(eng, n)
                if tail:
                    pe_tail_yT(eng, n - 1)
        k_tokens(1)
        if ahead:
            for t in range(NT):
                if tail and t == 0:
                    s_af.wait(eng, n - 1)
                pe_X(eng, n + 1, t)
        elif tail:
            s_af.wait(eng, n - 1)

        def scores(c):
            if c == 0:
                s_kx.wait(eng, n)
                s_rx.wait(eng, n)
                s_kl.wait(eng, n)
            for x in range(2):
                s_am.wait(eng, n, 2 * (c - 1) + x + 1) if c else None
                for gg in range(2):
                    g = 2 * x + gg
                    for i, (a, b) in enumerate(PASSES):
                        mm = eng.matmul(sc[:, x, gg * BT:(gg + 1) * BT],
                                        kx[:, G * a + g, c, :, :].rearrange("p a j -> p (a j)"),
                                        rx[:, b, g, :, Q * c:Q * c + Q], start=(i == 0), stop=(i == 2))
                s_sc.done(mm)

        def att_v(c):
            t, cc = c // 2, c % 2
            out = Y[Q * cc:Q * cc + Q, 0, :]
            if cc == 0:
                s_y.wait(eng, n, t) if t else s_vl.wait(eng, n, 1)
                s_vbd[t].wait(eng, n)
            s_al.wait(eng, n, 2 * c + 2)
            for q in range(16):
                for i, (a, b) in enumerate(PASSES):
                    mm = eng.matmul(out[:, 2 * N * q:2 * N * (q + 1)], att[:, cc, a, Q * q:Q * q + Q],
                                    vbd[:, t, cc, b, :, N * q:N * q + N],
                                    start=(i == 0), stop=(i == 2))
            s_av.done(mm)

        def from_state(c):
            t, cc = c // 2, c % 2
            if cc == 0:
                s_yi.wait(eng, n, t) if t else s_vl.wait(eng, n, 2)
            s_Sl.wait(eng, n, c) if c else s_Sl.wait(eng, n - 1)
            for g in range(G):
                for i, (a, b) in enumerate(PASSES):
                    mm = eng.matmul(Y[Q * cc:Q * cc + Q, 1, rows(g)], rT[:, a, g, Q * c:Q * c + Q],
                                    Shl[:, cc, b, rows(g)], start=(i == 0), stop=(i == 2))
            s_in.done(mm)

        def kv_sum(c):
            t, cc = c // 2, c % 2
            s_km.wait(eng, n, c) if c else s_km.wait(eng, n - 1)
            if cc == 0:
                s_vwl.wait(eng, n, t + 1)
                s_vwh.wait(eng, n, t + 1)
                s_kN.wait(eng, n, t + 1)
            part = slice(Q * cc, Q * cc + Q)
            for g in range(G):
                for i, (a, b) in enumerate(PASSES):
                    mm = eng.matmul(kvp[:, rows(g)], kN[part, t, a, rows(g)], vw[part, t, b, rows(g)],
                                    start=(i == 0), stop=(i == 2))
            s_kv.done(mm)

        def gate(half):
            if half == 0:
                mixed(3)
            if ahead:
                s_xT.wait(eng, n + 1, half + 1)
            s_pG.done(pe_project_T(eng, big[:, half, :], 3, 3, half))

        def out_tile(t):
            if tail:
                s_gT.wait(eng, n, t + 1)
                pe_tail_Wo(eng, n - 1, t)

        scores(0)
        kv_sum(0)
        gate(0)
        scores(1)
        att_v(0)
        from_state(0)
        gate(1)
        kv_sum(1)
        scores(2)
        att_v(1)
        from_state(1)
        out_tile(0)
        kv_sum(2)
        scores(3)
        att_v(2)
        from_state(2)
        out_tile(1)
        kv_sum(3)
        att_v(3)
        from_state(3)

    def dve_ln(eng, n):
        s_xa.wait(eng, n)
        for t in range(NT):
            s_bn.done(eng.bn_stats(bn[:, t, :], xa[:, t, :]))
            yield
        for t in range(NT):
            s_bn.wait_apart(eng, n, t + 1)
            s_bn.done(eng.bn_aggr(mv[:, t, :], bn[:, t, :]))
            yield
        s_bn.wait(eng, n)
        s_ln.done(eng.tensor_scalar(ln_a[:, :], mv[:, :, 1], LN_EPS, None, ALU.add))
        yield
        s_ln.wait(eng, n, 1)
        yield from rsqrt(eng, s_ln, n, ln_a[:, :], ln_r[:, :], ln_t[:, :], 1)
        s_ln.done(eng.scalar_tensor_tensor(out=ln_n[:, :], in0=mv[:, :, 0], scalar=-1.0, in1=ln_r[:, :],
                                           op0=ALU.mult, op1=ALU.mult))

    def dve_dx(eng, n):
        s_xT.wait(eng, n)
        s_carry.wait(eng, n)
        s_dx.done(eng.tensor_tensor(dx[:, :, :], xnT[:, :, 0:BT], xnT[:, :, 1:BT + 1], ALU.subtract))

    def dve_carry(eng, n):
        s_mix.wait(eng, n - 1)
        s_carry.done(eng.tensor_scalar(xnT[:, :, 0:1], xnT[:, :, BT:BT + 1], flag[:, bass.ds(n, 1)],
                                       None, ALU.mult))

    def dve_mix(eng, n, m):
        if m == 0:
            s_dx.wait(eng, n)
        s_ml.wait(eng, n, m - 1) if m >= 2 else s_ml.wait(eng, n - 1, m + 3)
        for g in range(G):
            last = eng.scalar_tensor_tensor(out=mixf[:, m % 2, g, :], in0=dx[:, g, :], scalar=maa[:, m, g:g + 1],
                                            in1=xnT[:, g, 1:BT + 1], op0=ALU.mult, op1=ALU.add)
            if g == G - 1:
                s_mix.done(last)
            yield

    def dve_lo(eng, projected, dst, half):
        g2 = slice(2 * half, 2 * half + 2)
        return eng.scalar_tensor_tensor(out=dst[:, 1, g2, :], in0=projected.rearrange("p (g t) -> p g t", g=2),
                                        scalar=1.0 / KS, in1=dst[:, 0, g2, :], op0=ALU.mult, op1=ALU.subtract)

    def dve_gated(eng, n):
        s_af.wait(eng, n)
        for t in range(NT):
            s_yg.done(eng.tensor_tensor(ygT[:, :, rows(t)], ygT[:, :, rows(t)], gT[:, :, rows(t)], ALU.mult))

    def dve_residual(eng, n, t):
        s_xr.wait(eng, n)
        s_Wo.wait(eng, n, t + 1)
        s_x1.done(eng.scalar_tensor_tensor(out=x1[:, t, :], in0=big[:, t, :], scalar=out_scale[:, 0:1],
                                           in1=x1[:, t, :], op0=ALU.mult, op1=ALU.add))

    def dve_variance(eng, n, t):
        s_sq.wait(eng, n, t + 1)
        s_gs.done(eng.tensor_reduce(gn_s[:, t, :], ysq[:, :].rearrange("p (h d) -> p h d", h=H), AX.X, ALU.add))

    def dve_normalize(eng, n):
        dve_variance(eng, n, 1)
        yield
        s_gs.wait(eng, n)
        s_gn.done(eng.tensor_scalar(gn_a[:, :, :], gn_s[:, :, :], 1.0 / N, gn_eps[:, 0:1], ALU.mult, ALU.add))
        yield
        s_gn.wait(eng, n, 1)
        yield from rsqrt(eng, s_gn, n, gn_a[:, :, :], gn_r[:, :, :], gn_t[:, :, :], 1)
        for t in range(NT):
            s_yn.done(eng.tensor_tensor(y[:, t, :].rearrange("p (h d) -> p h d", h=H),
                                        y[:, t, :].rearrange("p (h d) -> p h d", h=H),
                                        gn_r[:, t, :].unsqueeze(2).to_broadcast([P, H, N]), ALU.mult))
            yield

    def dve_block(eng, n, tail, ahead):
        def r_lo(half):
            s_rh.wait(eng, n, half + 1)
            s_rl.done(dve_lo(eng, big[:, half, :], rT, half))

        def mix_and_k():
            yield from dve_mix(eng, n, 2)
            for half in range(2):
                yield
                yield
                s_kh.wait(eng, n, half + 1)
                s_kl.done(dve_lo(eng, sc[:, half, :], kT, half))
            yield from dve_mix(eng, n, 3)
            r_lo(0)

        chains = [mix_and_k()]
        if tail:
            chains.append(dve_normalize(eng, n - 1))
        if ahead:
            chains.insert(0, dve_ln(eng, n + 1))
        in_turn(*chains)
        def weigh(c):
            for x in range(2):
                s_sc.wait(eng, n, 2 * c + x + 1)
                s_al.wait(eng, n, 2 * c - 1 + x) if c else s_al.wait(eng, n - 1, 2 * NCH - 1 + x)
                s_am.done(eng.tensor_tensor(att32[:, x, :], sc[:, x, :],
                                            wmask[:, 8 * x:8 * x + 8, :].rearrange("p q i -> p (q i)"), ALU.mult))

        r_lo(1)
        for t in range(NT):
            s_pV.wait(eng, n, t + 1)
            s_vw.done(eng.tensor_tensor(vw32[:, t, :].rearrange("p (h d) -> p h d", h=H),
                                        Y[:, t, :].rearrange("p (h d) -> p h d", h=H),
                                        wk[:, :].unsqueeze(2).to_broadcast([P, H, N]), ALU.mult))
            if t:
                weigh(0)
            else:
                if ahead:
                    dve_carry(eng, n + 1)
                s_Sw.wait(eng, n - 1)
                s_wsf.done(eng.tensor_scalar(wsf[:, :], ws[:, :], flag[:, bass.ds(n + 1, 1)], None, ALU.mult))
                if tail:
                    dve_gated(eng, n - 1)
            s_vh.wait(eng, n, t + 1)
            for p in range(2):
                last = eng.scalar_tensor_tensor(
                    out=vN[:, t, 1, p, :].rearrange("p (q d) -> p q d", d=N),
                    in0=Y[:, t, :].rearrange("p (q a d) -> p a q d", a=2, d=N)[:, p], scalar=1.0 / KS,
                    in1=vN[:, t, 0, p, :].rearrange("p (q d) -> p q d", d=N), op0=ALU.mult, op1=ALU.subtract)
            s_vl.done(last)

        def weights_lo(c):
            for x in range(2):
                s_ah.wait(eng, n, 2 * c + x + 1)
                s_al.done(eng.tensor_tensor(att[:, c % 2, 1, C * x:C * x + C], att32[:, x, :],
                                            att[:, c % 2, 0, C * x:C * x + C], ALU.subtract))

        def state(c):
            s_kv.wait(eng, n, c + 1)
            out, src = (b[:, :].rearrange("p (g c) -> p g c", g=G) for b in (kv, kvp))
            mask = headmask[:, :].unsqueeze(1).to_broadcast([P, G, P])
            if c < NCH - 1:
                s_km.done(eng.tensor_tensor(out, src, mask, ALU.mult))
            else:
                s_km.done(eng.scalar_tensor_tensor(out=out, in0=src, scalar=flag[:, bass.ds(n + 1, 1)], in1=mask,
                                                   op0=ALU.mult, op1=ALU.mult))
            s_km.wait(eng, n, c + 1)
            s_Sw.wait(eng, n, c) if c else s_Sw.wait(eng, n - 1)
            s_Sl.wait(eng, n, c) if c else s_Sl.wait(eng, n - 1)
            s_S.done(eng.tensor_tensor(S[:, :], kv[:, :], Sw[:, :], ALU.add))

        def gate(half):
            s_tg.wait(eng, n, half + 1)
            g2 = slice(2 * half, 2 * half + 2)
            s_gT.done(eng.scalar_tensor_tensor(out=gT[:, g2, :], in0=tg[:, half, :].rearrange("p (g t) -> p g t", g=2),
                                               scalar=1.0, in1=big[:, half, :].rearrange("p (g t) -> p g t", g=2),
                                               op0=ALU.add, op1=ALU.mult))

        def take_y(t):
            s_in.wait(eng, n, 2 * t + 2)
            s_av.wait(eng, n, 2 * t + 2)
            s_yi.done(eng.tensor_tensor(yi[:, :].rearrange("p (h d) -> p h d", h=H),
                                        Y[:, 1, :].rearrange("p (h d) -> p h d", h=H),
                                        wb[:, :].unsqueeze(2).to_broadcast([P, H, N]), ALU.mult))
            s_yi.wait(eng, n, t + 1)
            s_yT.wait(eng, n - 1)
            s_y.done(eng.tensor_tensor(y[:, t, :], Y[:, 0, :], yi[:, :], ALU.add))

        if ahead:
            dve_dx(eng, n + 1)
        weights_lo(0)
        if ahead:
            in_turn(dve_mix(eng, n + 1, 0))
        state(0)
        weigh(1)
        gate(0)
        weights_lo(1)
        if ahead:
            in_turn(dve_mix(eng, n + 1, 1))
        state(1)
        weigh(2)
        gate(1)
        weights_lo(2)
        take_y(0)
        if tail:
            dve_residual(eng, n - 1, 0)
        state(2)
        weigh(3)
        dve_variance(eng, n, 0)
        weights_lo(3)
        if tail:
            dve_residual(eng, n - 1, 1)
        state(3)
        take_y(1)

    def act_norm(eng, n):
        s_ln.wait(eng, n)
        for t in range(NT):
            s_xn.done(eng.activation(xa[:, t, :], xa[:, t, :], ACT.Identity, bias=ln_n[:, t:t + 1],
                                     scale=ln_r[:, t:t + 1]))

    def act_xT(eng, n):
        s_dx.wait(eng, n - 1)
        s_mix.wait(eng, n - 1)
        s_carry.wait(eng, n)
        for t in range(NT):
            s_X.wait(eng, n, t + 1)
            s_xT.done(eng.activation(xnT[:, :, 1 + P * t:1 + P * t + P],
                                     big[:, t, :].rearrange("p (g t) -> p g t", g=G), ACT.Copy))

    def act_mix_hi(eng, n, m):
        s_mix.wait(eng, n, m + 1)
        (s_pK, s_pR, s_pV, s_pG)[m].wait(eng, n - 1)
        s_mh.done(eng.activation(mix[:, m, 0, :, :], mixf[:, m % 2, :, :], ACT.Copy))

    def act_gated(eng, n):
        s_yT.wait(eng, n)
        for g in range(G):
            s_af.done(eng.activation(ygT[:, g, :].rearrange("p (t i) -> p t i", t=NT), big[:, :, rows(g)],
                                     ACT.Identity, bias=bet[:, g:g + 1], scale=gam[:, g:g + 1]))

    def act_gated_hi(eng, n):
        for t in range(NT):
            s_yg.wait(eng, n, t + 1)
            s_ygh.done(eng.activation(yg[:, 0, :, rows(t)], ygT[:, :, rows(t)], ACT.Copy))

    def act_block(eng, n, tail, ahead):
        def project_hi(projected, done, dst, half, src):
            projected.wait(eng, n, half + 1)
            done.done(eng.activation(dst[:, 0, 2 * half:2 * half + 2, :],
                                     src[:, half, :].rearrange("p (g t) -> p g t", g=2), ACT.Copy, scale=1.0 / KS))

        def k_tokens(t):
            s_kt.wait(eng, n, t + 1)
            s_kv.wait(eng, n - 1)
            s_kN.done(eng.activation(kN[:, t, :, :], trp[:, :].rearrange("p (a c) -> p a c", a=2), ACT.Copy))

        def v_hi(t):
            s_vbd[t].wait(eng, n - 1)
            s_vw.wait(eng, n, t + 1)
            s_vh.done(eng.activation(vN[:, t, 0, :, :].rearrange("p a (q d) -> p a q d", d=N),
                                     Y[:, t, :].rearrange("p (q a d) -> p a q d", a=2, d=N), ACT.Copy,
                                     scale=1.0 / KS))

        def vw_hi(t):
            s_kv.wait(eng, n - 1)
            s_vwh.done(eng.activation(vw[:, t, 0, :], vw32[:, t, :], ACT.Copy))

        s_kx.wait(eng, n - 1)
        s_kt.wait(eng, n - 1)
        for half in range(2):
            project_hi(s_pK, s_kh, kT, half, sc)
        act_mix_hi(eng, n, 2)
        s_rx.wait(eng, n - 1)
        s_in.wait(eng, n - 1)
        for half in range(2):
            project_hi(s_pR, s_rh, rT, half, big)
        act_mix_hi(eng, n, 3)
        if ahead:
            act_norm(eng, n + 1)
        if tail:
            s_ml.wait(eng, n, 1)
            act_gated(eng, n - 1)
        k_tokens(0)
        v_hi(0)
        vw_hi(0)
        if ahead:
            act_xT(eng, n + 1)
        v_hi(1)
        vw_hi(1)
        def weights_hi(c):
            s_av.wait(eng, n, c - 1) if c >= 2 else s_av.wait(eng, n - 1, NCH - 1 + c)
            for x in range(2):
                s_am.wait(eng, n, 2 * c + x + 1)
                s_ah.done(eng.activation(att[:, c % 2, 0, C * x:C * x + C], att32[:, x, :], ACT.Copy))

        def state_hi(c):
            b = (c + 1) % 2
            s_S.wait(eng, n, c + 1)
            s_in.wait(eng, n, c) if c else s_in.wait(eng, n - 1)
            s_Sh.done(eng.activation(Shl[:, b, 0, :], S[:, :], ACT.Copy))

        def gate(half):
            s_pG.wait(eng, n, half + 1)
            s_t.wait(eng, 15)
            s_gT.wait(eng, n - 1)
            s_tg.done(eng.activation(tg[:, half, :], big[:, half, :], ACT.Tanh, scale=half_rho_g[:, 0:1]))

        def square(t):
            s_y.wait(eng, n, t + 1)
            s_gs.wait(eng, n, t) if t else s_gs.wait(eng, n - 1)
            s_sq.done(eng.activation(ysq[:, :], y[:, t, :], ACT.Square))

        weights_hi(0)
        k_tokens(1)
        if tail:
            act_gated_hi(eng, n - 1)
        if ahead:
            act_mix_hi(eng, n + 1, 0)
        state_hi(0)
        gate(0)
        weights_hi(1)
        if ahead:
            act_mix_hi(eng, n + 1, 1)
        gate(1)
        state_hi(1)
        weights_hi(2)
        square(0)
        state_hi(2)
        weights_hi(3)
        state_hi(3)
        square(1)

    def pool_mix_lo(eng, n, m):
        s_mh.wait(eng, n, m + 1)
        s_ml.done(eng.tensor_tensor(mix[:, m, 1, :, :], mixf[:, m % 2, :, :], mix[:, m, 0, :, :], ALU.subtract))

    def pool_gated_lo(eng, n):
        for t in range(NT):
            s_ygh.wait(eng, n, t + 1)
            s_ygl.done(eng.tensor_tensor(yg[:, 1, :, rows(t)], ygT[:, :, rows(t)], yg[:, 0, :, rows(t)],
                                         ALU.subtract))

    def pool_block(eng, n, tail, ahead):
        def decay_state(c):
            s_S.wait(eng, n, c + 1)
            decay = ws
            if c == NCH - 2:
                s_wsf.wait(eng, n)
                decay = wsf
            s_Sw.done(eng.tensor_tensor(Sw[:, :].rearrange("p (g c) -> p g c", g=G),
                                        S[:, :].rearrange("p (g c) -> p g c", g=G),
                                        decay[:, :].unsqueeze(2).to_broadcast([P, G, P]), ALU.mult))

        def state_lo(c):
            s_Sh.wait(eng, n, c + 1)
            b = (c + 1) % 2
            s_Sl.done(eng.tensor_tensor(Shl[:, b, 1, :], S[:, :], Shl[:, b, 0, :], ALU.subtract))

        pool_mix_lo(eng, n, 2)
        pool_mix_lo(eng, n, 3)
        for t in range(NT):
            s_vwh.wait(eng, n, t + 1)
            s_vwl.done(eng.tensor_tensor(vw[:, t, 1, :], vw32[:, t, :], vw[:, t, 0, :], ALU.subtract))
        if tail:
            pool_gated_lo(eng, n - 1)
        for c in range(NCH):
            if ahead and c < 2:
                pool_mix_lo(eng, n + 1, c)
            state_lo(c)
            decay_state(c)

    def sp_block(eng, n, tail, ahead, load):
        s_sc.wait_apart(eng, n - 1)
        s_kl.wait_apart(eng, n)
        for b in range(8):
            p = b % 2
            s_kx.done(eng.dma_start(kx[N * b:N * b + N, :, :, p, :],
                                    kT[N * b:N * b + N, :, :, :].rearrange("p a g (c j) -> p (a g) c j", j=Q)))
        s_rl.wait_apart(eng, n)
        for q in range(4):
            s_rx.done(eng.dma_start(rx[32 * q:32 * q + 32, :, :, q, :], rT[32 * q:32 * q + 32, :, :, :]))
        for t in range(NT):
            s_vl.wait_apart(eng, n, t + 1)
            s_av.wait_apart(eng, n - 1, 2 * t + 2)
            for c in range(2):
                for p in range(2):
                    s_vbd[t].done(eng.dma_start(vbd[Q * p:Q * p + Q, t, c, :, p, :], vN[Q * c:Q * c + Q, t, :, p, :]))
        if load:
            s_X.wait_apart(eng, n + 1)
            s_xa.done(eng.dma_start(xa[:, :, :], x_rows(x, n + 2)))
        if tail:
            s_x1.wait_apart(eng, n - 1)
            s_st.done(eng.dma_start(x_rows(x1_out, n - 1), x1[:, :, :]))
            s_st.wait_apart(eng, n - 1)
        s_xr.done(eng.dma_start(x1[:, :, :], x_rows(x, n)))

    def every_block(eng, block_fn, extra=False):
        if extra:
            block_fn(eng, 0, False, True, True)
            with eng.Fori(1, nb - 2) as n:
                block_fn(eng, n, True, True, True)
            block_fn(eng, nb - 2, True, True, False)
            block_fn(eng, nb - 1, True, False, False)
        else:
            block_fn(eng, 0, False, True)
            with eng.Fori(1, nb - 1) as n:
                block_fn(eng, n, True, True)
            block_fn(eng, nb - 1, True, False)

    def pe_start(eng):
        s_ident.wait(eng, 0)
        for t in range(NT):
            pe_X(eng, 0, t)

    def dve_start(eng):
        in_turn(dve_ln(eng, 0))
        s_carry.done(eng.memset(xnT[:, :, 0:1], 0.0))
        s_maa.wait(eng, 0)
        dve_dx(eng, 0)
        for m in range(2):
            in_turn(dve_mix(eng, 0, m))

    def act_start(eng):
        act_norm(eng, 0)
        act_xT(eng, 0)
        for m in range(2):
            act_mix_hi(eng, 0, m)

    def pool_start(eng):
        for m in range(2):
            pool_mix_lo(eng, 0, m)

    with ExitStack() as own:
        fifth = own.enter_context(nc.sbuf_tensor("fifth", [P, G, C], F32))
        wu = WeightUnits(nc, own, "a", weights, [store[:, k, :, :] for k in range(4)] + [fifth[:, :, :]],
                         [[0, 1, 2, 3, 4]], [2], V_)
        load_weights(nc, "a", wu, range(5), [WT[:, w, :, :, :] for w in range(5)], rho[:, :], scl[:, :],
                     ident16[:, :], centring[:, :], load_first, load_last, s_const,
                     aside=(0, dict(vector=dve_start, scalar=act_start, tensor=pe_start, gpsimd=pool_start)))

    kT = sb("kT", [P, 2, G, BT], F16)
    rT = sb("rT", [P, 2, G, BT], F16)
    flat = store[:, :, :, :].rearrange("p u b c -> p (u b c)").bitcast(F16)
    n_kx, n_rx, n_vbd = 2 * G * BT * 2, 2 * G * 4 * BT, NT * 2 * 2 * C
    kx = flat[:, 0:n_kx].rearrange("p (a c b j) -> p a c b j", a=2 * G, c=NCH, b=2)
    rx = flat[:, n_kx:n_kx + n_rx].rearrange("p (a g q t) -> p a g q t", a=2, g=G, q=4)
    vbd = flat[:, n_kx + n_rx:n_kx + n_rx + n_vbd].rearrange("p (t c a b d) -> p t c a b d", t=NT, c=2, a=2, b=2)
    kN = sb("kN", [P, NT, 2, C], F16)
    vN = sb("vN", [P, NT, 2, 2, C // 2], F16)
    vw32 = sb("vw32", [P, NT, C])
    vw = sb("vw", [P, NT, 2, C], F16)
    tg = sb("tg", [P, NT, C])
    gT = sb("gT", [P, G, BT])
    att32 = sb("att32", [P, 2, C])
    att = sb("att", [P, 2, 2, 2 * C], F16)
    kv = sb("kv", [P, C])
    S = sb("S", [P, C])
    Sw = sb("Sw", [P, C])
    Shl = sb("Shl", [P, 2, 2, C], F16)
    yi = sb("yi", [P, C])
    y = sb("y", [P, NT, C])
    ysq = sb("ysq", [P, C])
    gn_s, gn_a, gn_r, gn_t = (sb(f"gn_{c}", [P, NT, H]) for c in "sart")
    ygT = sb("ygT", [P, G, BT])
    yg = sb("yg", [P, 2, G, BT], F16)
    x1 = sb("x1", [P, NT, C])

    sc = ps("sc", [P, 2, C])
    Y = ps("Y", [P, 2, C])
    kvp = ps("kvp", [P, C])
    trp = ps("trp", [P, 2 * C], F16)

    with nc.Block() as block:
        @block.sync
        def _(eng):
            s_X.wait(eng, 0)
            s_xa.done(eng.dma_start(xa[:, :, :], x_rows(x, 1)))
            s_zero.wait(eng, 2)
            every_block(eng, sp_block, True)
            s_av.wait(eng, nb - 1)
            for u in next_units.rounds[0]:
                next_units.load(eng, u)
            s_x1.wait(eng, nb - 1)
            s_st.done(eng.dma_start(x_rows(x1_out, nb - 1), x1[:, :, :]))
            s_st.wait(eng, nb - 1)

        @block.tensor
        def _(eng):
            s_zero.wait(eng, 1)
            every_block(eng, pe_block)
            s_x1.wait(eng, nb - 2)
            pe_tail_yT(eng, nb - 1)
            for t in range(NT):
                pe_tail_Wo(eng, nb - 1, t)

        @block.vector
        def _(eng):
            dve_tables(eng)
            every_block(eng, dve_block)
            in_turn(dve_normalize(eng, nb - 1))
            dve_gated(eng, nb - 1)
            for t in range(NT):
                dve_residual(eng, nb - 1, t)
            next_units.dve_squares(eng, 0)

        @block.scalar
        def _(eng):
            act_tables(eng)
            every_block(eng, act_block)
            s_ygl.wait(eng, nb - 2)
            act_gated(eng, nb - 1)
            act_gated_hi(eng, nb - 1)
            next_units.act_squares(eng, 0)

        @block.gpsimd
        def _(eng):
            s_zero.done(eng.memset(Sw[:, :], 0.0))
            s_zero.done(eng.memset(Shl[:, 0, :, :].rearrange("p a c -> p (a c)").bitcast(F32), 0.0))
            s_zero.done(eng.memset(store[:, :, :, :].rearrange("p u b c -> p (u b c)"), 0.0))
            s_x.wait(eng, NT * 8 + 2)
            every_block(eng, pool_block)
            pool_gated_lo(eng, nb - 1)


def ffn(nc, ctx, xio_in, out, bias0, bias1, consts, nb, store, wu):

    def sb(name, shape, dt=F32):
        return ctx.enter_context(nc.sbuf_tensor(name, shape, dt))

    def ps(name, shape, dt=F32):
        return ctx.enter_context(nc.psum_tensor(name, shape, dt))

    s_passed = ctx.enter_context(nc.semaphore("f_passed"))

    def step(name, per, unit=1):
        return Step(nc, ctx, name, per, unit, s_passed)

    def rows(t):
        return slice(P * t, P * t + P)

    NH = HID // P
    ident16 = sb("f_ident16", [P, P], F16)
    W0T = sb("W0T", [P, 2, G, HID], F16)
    W1T = sb("W1T", [P, 2, NH, C], F16)
    rho = sb("f_rho", [P, 2])
    scl = sb("f_scl", [P, 2])
    b0 = sb("b0", [P, NH])
    b1 = sb("b1", [P, C])
    f_const = step("f_const", 1, 16)
    f_b1 = step("f_b1", 1, 16)
    f_scale = step("f_scale", 1)
    x1 = sb("f_x1", [P, FN, C])
    s_ld = step("f_ld", 1, 16)

    def blk(x, n):
        return x[bass.ds(n * FN, FN), :, :].rearrange("t p c -> p t c")

    def load_first(eng):
        s_ld.done(eng.dma_start(x1[:, :, :], blk(xio_in, 0)))
        f_const.done(eng.dma_start(ident16[:, :], consts["ident16"]))
        f_const.done(eng.dma_start(b0[:, :], bias0.rearrange("(g p) -> p g", p=P), allow_slow_non_contiguous=True))

    def load_last(eng):
        f_b1.done(eng.dma_start(b1[:, :], bias1.partition_broadcast(P)))
        f_b1.wait(eng, 0)

    places = [W0T[:, :, :, C * u:C * u + C] for u in range(4)] + [W1T[:, :, G * u:G * u + G, :] for u in range(4)]
    bn = sb("f_bn", [P, FN, 6])
    mv = sb("f_mv", [P, FN, 2])
    ln_a, ln_r, ln_t, ln_n = (sb(f"f_ln_{c}", [P, FN]) for c in "artn")
    xh = sb("f_xh", [P, FN, C], F16)
    xT = sb("f_xT", [P, G, FT], F16)
    trp = ps("f_trp", [P, 2, 2 * C], F16)

    s_rs = step("f_rs", 1, 16)
    s_st = step("f_st", 1, 16)
    s_bn = step("f_sbn", 2 * FN)
    s_ln = step("f_sln", 2 + RSQRT_STEPS)
    s_xh = step("f_sxh", FN)
    s_tr = step("f_str", 2)
    s_xT = step("f_sxT", 2)
    s_up = step("f_sup", NH)
    s_h = step("f_sh", NH)
    s_dn = step("f_sdn", FN)
    s_e = step("f_se", FN)
    s_o = step("f_so", FN)

    def sp_block(eng, n, load):
        s_o.wait_apart(eng, n - 1)
        s_rs.done(eng.dma_start(xr[:, :, :], blk(xio_in, n)))
        if load:
            s_xh.wait_apart(eng, n + 1)
            s_ld.done(eng.dma_start(x1[:, :, :], blk(xio_in, n + 2)))
        s_o.wait_apart(eng, n)
        s_st.done(eng.dma_start(blk(out, n), o[:, :, :]))

    def dve_ln(eng, n):
        s_ld.wait(eng, n)
        for t in range(FN):
            s_bn.done(eng.bn_stats(bn[:, t, :], x1[:, t, :]))
        for t in range(FN):
            s_bn.wait_apart(eng, n, t + 1)
            s_bn.done(eng.bn_aggr(mv[:, t, :], bn[:, t, :]))
        s_bn.wait(eng, n)
        s_ln.done(eng.tensor_scalar(ln_a[:, :], mv[:, :, 1], LN_EPS, None, ALU.add))
        s_ln.wait(eng, n, 1)
        yield from rsqrt(eng, s_ln, n, ln_a[:, :], ln_r[:, :], ln_t[:, :], 1)
        s_ln.done(eng.scalar_tensor_tensor(out=ln_n[:, :], in0=mv[:, :, 0], scalar=-1.0, in1=ln_r[:, :],
                                           op0=ALU.mult, op1=ALU.mult))

    def dve_xT(eng, n):
        s_up.wait(eng, n - 1)
        for k in range(2):
            s_tr.wait(eng, n, k + 1)
            s_xT.done(eng.tensor_copy(xT[:, 2 * k:2 * k + 2, :], trp[:, k, :].rearrange("p (g t) -> p g t", g=2)))

    def dve_block(eng, n, ahead):
        if ahead:
            in_turn(dve_ln(eng, n + 1))
            dve_xT(eng, n + 1)
        for t in range(FN):
            s_dn.wait(eng, n, t + 1)
            s_o.wait(eng, n - 1, t + 1)
            s_e.done(eng.scalar_tensor_tensor(out=e16[:, t, :], in0=down[:, t % 2, :], scalar=rho[:, 1:2],
                                              in1=b1[:, :], op0=ALU.mult, op1=ALU.add))

    def act_norm(eng, n):
        s_ln.wait(eng, n)
        s_tr.wait(eng, n - 1)
        for t in range(FN):
            s_xh.done(eng.activation(xh[:, t, :], x1[:, t, :], ACT.Identity, bias=ln_n[:, t:t + 1],
                                     scale=ln_r[:, t:t + 1]))

    def act_block(eng, n, ahead):
        s_dn.wait(eng, n - 1)
        for k in range(NH):
            if k == NH // 2 and ahead:
                act_norm(eng, n + 1)
            s_up.wait(eng, n, k + 1)
            s_h.done(eng.activation(hT[:, k, :], up[:, k % 4, :], ACT.Gelu, bias=b0[:, k:k + 1], scale=rho[:, 0:1]))

    def pe_transposes(eng, n):
        s_xh.wait(eng, n)
        for k in range(2):
            s_xT.wait(eng, n - 1, k + 1)
            for gg in range(2):
                for t in range(FN):
                    tr = eng.transpose(trp[:, k, gg * FT + P * t:gg * FT + P * t + P], xh[:, t, rows(2 * k + gg)],
                                       ident16[:, :])
            s_tr.done(tr)

    def pe_block(eng, n, ahead):
        s_xT.wait(eng, n)
        for k in range(NH):
            s_h.wait(eng, n, k - 3) if k >= 4 else s_h.wait(eng, n - 1, NH - 3 + k)
            for kk in range(G):
                for a in range(2):
                    mm = eng.matmul(up[:, k % 4, :], W0T[:, a, kk, rows(k)], xT[:, kk, :],
                                    start=(kk == 0 and a == 0), stop=(kk == G - 1 and a == 1))
            s_up.done(mm)
        if ahead:
            pe_transposes(eng, n + 1)
        for t in range(FN):
            s_e.wait(eng, n, t - 1) if t >= 2 else s_e.wait(eng, n - 1, FN - 1 + t)
            s_h.wait(eng, n)
            for k in range(NH):
                for a in range(2):
                    mm = eng.matmul(down[:, t % 2, :], hT[:, k, rows(t)], W1T[:, a, k, :],
                                    start=(k == 0 and a == 0), stop=(k == NH - 1 and a == 1))
            s_dn.done(mm)

    def pool_block(eng, n, ahead):
        s_rs.wait(eng, n)
        s_st.wait(eng, n - 1)
        for t in range(FN):
            s_e.wait(eng, n, t + 1)
            s_o.done(eng.tensor_tensor(o[:, t, :], e16[:, t, :], xr[:, t, :], ALU.add))

    def every_block(eng, fn):
        fn(eng, 0, True)
        with eng.Fori(1, nb - 1) as n:
            fn(eng, n, True)
        fn(eng, nb - 1, False)

    load_weights(nc, "f", wu, [u // 4 for u in range(8)], places, rho[:, :], scl[:, :], ident16[:, :], None,
                 load_first, load_last, f_const, len(wu.rounds[0]),
                 (1, dict(vector=lambda eng: in_turn(dve_ln(eng, 0)), scalar=lambda eng: act_norm(eng, 0),
                          tensor=lambda eng: pe_transposes(eng, 0))))

    hT = store[:, 0:2, :, :].rearrange("p u b c -> p (u b c)").bitcast(F16).rearrange("p (k t) -> p k t", t=FT)
    e16 = sb("f_e16", [P, FN, C], F16)
    o = store[:, 2, :, :]
    xr = store[:, 3, :, :]

    up = ps("up_ps", [P, 4, C])
    down = ps("down_ps", [P, 2, C])

    with nc.Block() as block:
        @block.sync
        def _(eng):
            s_xh.wait(eng, 0)
            s_ld.done(eng.dma_start(x1[:, :, :], blk(xio_in, 1)))
            sp_block(eng, 0, True)
            with eng.Fori(1, nb - 2) as n:
                sp_block(eng, n, True)
            sp_block(eng, nb - 2, False)
            sp_block(eng, nb - 1, False)
            s_st.wait(eng, nb - 1)

        @block.vector
        def _(eng):
            f_scale.done(eng.tensor_scalar(rho[:, :], rho[:, :], 1.0 / KS, None, ALU.mult))
            f_scale.wait(eng, 0)
            dve_xT(eng, 0)
            every_block(eng, dve_block)

        @block.scalar
        def _(eng):
            f_scale.wait(eng, 0)
            every_block(eng, act_block)

        @block.tensor
        def _(eng):
            every_block(eng, pe_block)

        @block.gpsimd
        def _(eng):
            every_block(eng, pool_block)


def build(nc, a, consts, x1, out):
    tiles = lambda v: v.rearrange("b (t p) c -> (b t) p c", p=P)
    ntok = a["L0_attn_x"].shape[0] * a["L0_attn_x"].shape[1]
    W0, W1 = a["L0_ffn_W0"], a["L0_ffn_W1"]
    with ExitStack() as both:
        store = both.enter_context(nc.sbuf_tensor("store", [P, 4, G, C], F32))
        sources = [W0[C * u:C * u + C, :] for u in range(4)] + [W1[:, C * u:C * u + C] for u in range(4)]
        wu = WeightUnits(nc, both, "f", sources, [store[:, k, :, :] for k in range(4)], [[0, 1, 2, 3], [4, 5, 6, 7]],
                         [1, 2])
        with ExitStack() as ctx:
            attention(nc, ctx, tiles(a["L0_attn_x"]), x1,
                      [a[f"L0_attn_time_maa_{m}"] for m in "krvg"], [a[f"L0_attn_W{m}"] for m in "krvgo"],
                      a["L0_attn_time_decay"], a["L0_attn_time_faaaa"], a["L0_attn_gamma"], a["L0_attn_beta"],
                      consts, ntok // BT, store, wu)
        with ExitStack() as ctx:
            ffn(nc, ctx, x1, tiles(out), a["L0_ffn_bias0"], a["L0_ffn_bias1"], consts, ntok // FT, store, wu)


_INS = ['L0_attn_x', 'L0_attn_time_maa_k', 'L0_attn_time_maa_v', 'L0_attn_time_maa_r', 'L0_attn_time_maa_g',
        'L0_attn_time_decay', 'L0_attn_time_faaaa', 'L0_attn_Wr', 'L0_attn_Wk', 'L0_attn_Wv', 'L0_attn_Wg',
        'L0_attn_Wo', 'L0_attn_gamma', 'L0_attn_beta', 'L0_ffn_W0', 'L0_ffn_bias0', 'L0_ffn_W1', 'L0_ffn_bias1']


def constants():
    r = np.arange(P)
    i, j = np.arange(Q)[None, :], (r % Q)[:, None]
    same_head = (r[:, None] // N == r[None, :] // N).astype(np.float32)
    return {
        "ident": np.eye(P, dtype=np.float32),
        "ident16": np.eye(P, dtype=np.float16),
        "centring": (np.eye(P) - same_head / N).astype(np.float32),
        "headmask": same_head,
        "dist": np.maximum(i - j - 1, 0).astype(np.float32),
        "after": ((i > j) * ATT_S).astype(np.float32),
        "same": ((i == j) * ATT_S).astype(np.float32),
        "ages": np.stack([-(r % Q), -(Q - 1 - r % Q)], 1).astype(np.float32),
    }


def kernel(**inputs):
    import concourse.bacc as bacc
    from concourse.bass_utils import run_bass_kernel_spmd

    nc = bacc.Bacc("TRN2", target_bir_lowering=False, num_devices=1)
    arrays, aps, consts = {}, {}, {}
    for name in _INS:
        v = np.ascontiguousarray(inputs[name])
        arrays[f"in_{name}"] = v
        aps[name] = nc.dram_tensor(f"in_{name}", v.shape, mybir.dt.from_np(v.dtype), kind="ExternalInput").ap()
    for name, v in constants().items():
        v = np.ascontiguousarray(v)
        arrays[f"const_{name}"] = v
        consts[name] = nc.dram_tensor(f"const_{name}", v.shape, mybir.dt.from_np(v.dtype), kind="ExternalInput").ap()
    shape = inputs["L0_attn_x"].shape
    tiles = shape[0] * shape[1] // P
    x1 = nc.dram_tensor("x1_dram", (tiles, P, C), F32, kind="Internal").ap()
    out = nc.dram_tensor("out", shape, F32, kind="ExternalOutput").ap()
    build(nc, aps, consts, x1, out)
    r = run_bass_kernel_spmd(nc, [arrays], core_ids=[0])
    return r.results[0]["out"]
```
